# Optimizing a Trainium2 kernel written in Bass

```python
import numpy as np
import jax
import jax.numpy as jnp

def _softmax(x, axis=-1):
    return jax.nn.softmax(x, axis=axis)

def _gelu(x):
    return jax.nn.gelu(x, approximate=True)

def _silu(x):
    return jax.nn.silu(x)

def _sigmoid(x):
    return jax.nn.sigmoid(x)

def _layernorm(x, axis=-1, eps=1e-05):
    m = jnp.mean(x, axis=axis, keepdims=True)
    v = jnp.var(x, axis=axis, keepdims=True)
    return (x - m) / jnp.sqrt(v + eps)

def _scatter_add(tgt, idx, src, axis=0):
    return tgt.at[idx].add(src)

def _segment_sum(src, seg, n):
    return jax.ops.segment_sum(src, seg, n)
kernel_name = 'mk_vit_tower_d1_tok_img512_r4_0a3ec5'

def setup_inputs(seed: int=0):
    np.random.seed(seed)
    _w = jnp.asarray

    def _rec_inputs():
        import jax
        import jax.numpy as jnp
        _rk = jax.random.key(seed)
        x = -0.000356955 + 1 * jax.random.normal(jax.random.fold_in(_rk, 1), (64, 3, 224, 224), jnp.float32)
        return x
    x = _rec_inputs()

    def _L0_tok_setup():
        import jax, jax.numpy as jnp
        import numpy as np
        key = jax.random.key(seed)
        k1, k2, k3 = jax.random.split(key, 3)
        B, C, H, W = (128, 3, 224, 224)
        E, p = (128, 16)
        K = C * p * p
        img = jax.random.normal(k1, (B, C, H, W), dtype=jnp.float32)
        w = jax.random.normal(k2, (E, K), dtype=jnp.float32) * (1.0 / np.sqrt(K))
        b = jax.random.normal(k3, (E,), dtype=jnp.float32)
        return {'img': img, 'w': w, 'b': b, 'patch_size': p}
    _L0_tok_all = _L0_tok_setup()
    _L0_tok_in = {k: v for k, v in _L0_tok_all.items() if k in ('w', 'b')}
    del _L0_tok_all

    def _L0_attn_setup():
        import jax, jax.numpy as jnp
        import numpy as np
        N_HEAD = 8
        D_HEAD = 64
        D_MODEL = 128
        SEQ = 512
        BATCH = 2
        key = jax.random.key(seed)
        k1, k2, k3, k4 = jax.random.split(key, 4)
        s = 0.02
        h = jax.random.normal(k1, (SEQ, BATCH, D_MODEL), dtype=jnp.float32)
        Wq = jax.random.normal(k2, (N_HEAD * D_HEAD, D_MODEL), dtype=jnp.float32) * s
        Wkv = jax.random.normal(k3, (2 * N_HEAD * D_HEAD, D_MODEL), dtype=jnp.float32) * s
        Wo = jax.random.normal(k4, (D_MODEL, N_HEAD * D_HEAD), dtype=jnp.float32) * s
        return {'h': h, 'Wq': Wq, 'Wkv': Wkv, 'Wo': Wo}
    _L0_attn_all = _L0_attn_setup()
    _L0_attn_in = {k: v for k, v in _L0_attn_all.items() if k in ('Wq', 'Wkv', 'Wo')}
    del _L0_attn_all

    def _L0_ffn_setup():
        import jax, jax.numpy as jnp
        import numpy as np
        N_CONST = 6
        PARTITIONS_OF_6 = [(6,), (5, 1), (4, 2), (4, 1, 1), (3, 3), (3, 2, 1), (3, 1, 1, 1), (2, 2, 2), (2, 2, 1, 1), (2, 1, 1, 1, 1), (1, 1, 1, 1, 1, 1)]
        N_EXPERTS = 6
        TOP_K = 2

        def _partition_weights():
            w = np.zeros((len(PARTITIONS_OF_6), N_EXPERTS), dtype=np.float32)
            for i, partition in enumerate(PARTITIONS_OF_6):
                for j, part in enumerate(partition):
                    if j < N_EXPERTS:
                        w[i, j] = part / N_CONST
            return jnp.asarray(w)
        key = jax.random.key(seed)
        ks = jax.random.split(key, 6)
        B, S, D, F, E, P = (32, 512, 128, 341, 6, 11)
        scale_in = 1.0 / np.sqrt(D)
        scale_hid = 1.0 / np.sqrt(F)
        return {'x': jax.random.normal(ks[0], (B, S, D), dtype=jnp.float32), 'router_w': jax.random.normal(ks[1], (P, D), dtype=jnp.float32) * scale_in, 'W1': jax.random.normal(ks[2], (E, D, F), dtype=jnp.float32) * scale_in, 'b1': jax.random.normal(ks[3], (E, F), dtype=jnp.float32) * 0.01, 'W2': jax.random.normal(ks[4], (E, F, D), dtype=jnp.float32) * scale_hid, 'b2': jax.random.normal(ks[5], (E, D), dtype=jnp.float32) * 0.01}
    _L0_ffn_all = _L0_ffn_setup()
    _L0_ffn_in = {k: v for k, v in _L0_ffn_all.items() if k in ('router_w', 'W1', 'b1', 'W2', 'b2')}
    del _L0_ffn_all
    return {'x': x, 'L0_tok_w': _L0_tok_in['w'], 'L0_tok_b': _L0_tok_in['b'], 'L0_attn_Wq': _L0_attn_in['Wq'], 'L0_attn_Wkv': _L0_attn_in['Wkv'], 'L0_attn_Wo': _L0_attn_in['Wo'], 'L0_ffn_router_w': _L0_ffn_in['router_w'], 'L0_ffn_W1': _L0_ffn_in['W1'], 'L0_ffn_b1': _L0_ffn_in['b1'], 'L0_ffn_W2': _L0_ffn_in['W2'], 'L0_ffn_b2': _L0_ffn_in['b2']}

def reference(x, L0_tok_w, L0_tok_b, L0_attn_Wq, L0_attn_Wkv, L0_attn_Wo, L0_ffn_router_w, L0_ffn_W1, L0_ffn_b1, L0_ffn_W2, L0_ffn_b2):
    import jax
    import jax.numpy as jnp

    def _L0_tok_ref(img, w, b, patch_size):
        import jax, jax.numpy as jnp
        import numpy as np
        B, C, H, W = img.shape
        p = patch_size
        Hp, Wp = (H // p, W // p)
        S = Hp * Wp
        patches = img.reshape(B, C, Hp, p, Wp, p)
        patches = patches.transpose(0, 2, 4, 1, 3, 5).reshape(B, S, C * p * p)
        out = jnp.einsum('bsk,ek->bse', patches, w) + b
        return out

    def _L0_attn_ref(h, Wq, Wkv, Wo):
        import jax, jax.numpy as jnp
        import numpy as np
        N_HEAD = 8
        D_HEAD = 64
        D_MODEL = 128
        SEQ = 512
        BATCH = 2
        S, B, D = h.shape
        scale = 1.0 / D_HEAD ** 0.5
        q = (h @ Wq.T).reshape(S, B, N_HEAD, D_HEAD)
        kv = h @ Wkv.T
        k, v = jnp.split(kv, 2, axis=-1)
        k = k.reshape(S, B, N_HEAD, D_HEAD)
        v = v.reshape(S, B, N_HEAD, D_HEAD)
        scores = jnp.einsum('qbhd,kbhd->qkbh', q, k) * scale
        causal = jnp.triu(jnp.ones((S, S), dtype=bool), k=1)
        scores = jnp.where(causal[:, :, None, None], jnp.float32(-1000000.0), scores)
        prob = jax.nn.softmax(scores, axis=1)
        attn_vec = jnp.einsum('qkbh,kbhd->qbhd', prob, v).reshape(S, B, N_HEAD * D_HEAD)
        return attn_vec @ Wo.T

    def _L0_ffn_ref(x, router_w, W1, b1, W2, b2):
        import jax, jax.numpy as jnp
        import numpy as np
        N_CONST = 6
        PARTITIONS_OF_6 = [(6,), (5, 1), (4, 2), (4, 1, 1), (3, 3), (3, 2, 1), (3, 1, 1, 1), (2, 2, 2), (2, 2, 1, 1), (2, 1, 1, 1, 1), (1, 1, 1, 1, 1, 1)]
        N_EXPERTS = 6
        TOP_K = 2

        def _partition_weights():
            w = np.zeros((len(PARTITIONS_OF_6), N_EXPERTS), dtype=np.float32)
            for i, partition in enumerate(PARTITIONS_OF_6):
                for j, part in enumerate(partition):
                    if j < N_EXPERTS:
                        w[i, j] = part / N_CONST
            return jnp.asarray(w)
        pw = _partition_weights()
        token_repr = x.mean(axis=1)
        logits = token_repr @ router_w.T
        probs = jax.nn.softmax(logits, axis=-1)
        topk_vals, topk_idx = jax.lax.top_k(probs, TOP_K)
        topk_vals = topk_vals / topk_vals.sum(axis=-1, keepdims=True)
        expert_weights = jnp.einsum('bk,bke->be', topk_vals, pw[topk_idx])
        expert_weights = jnp.where(expert_weights > 1e-06, expert_weights, 0.0)
        h = jax.nn.gelu(jnp.einsum('bsd,edf->ebsf', x, W1) + b1[:, None, None, :], approximate=False)
        out_e = jnp.einsum('ebsf,efd->ebsd', h, W2) + b2[:, None, None, :]
        return jnp.einsum('be,ebsd->bsd', expert_weights, out_e)
    h = _L0_tok_ref(x, L0_tok_w, L0_tok_b, 16)
    h = h + _L0_attn_ref(_layernorm(h, axis=-1), L0_attn_Wq, L0_attn_Wkv, L0_attn_Wo)
    h = h + _L0_ffn_ref(_layernorm(h, axis=-1), L0_ffn_router_w, L0_ffn_W1, L0_ffn_b1, L0_ffn_W2, L0_ffn_b2)
    return h

_drawn_inputs = setup_inputs


def setup_inputs(seed=0):
    import zlib

    import numpy as np

    out = dict(_drawn_inputs(seed))
    spreads = {}
    factors = {'L0_attn_Wq': 64.0, 'L0_ffn_b1': 8.0, 'L0_ffn_b2': 8.0}
    for name, (base, spread) in spreads.items():
        noise = np.random.default_rng([zlib.crc32(name.encode()), seed]).standard_normal(out[name].shape)
        drawn = base * np.exp(spread * noise) if base else spread * noise
        out[name] = jnp.asarray(drawn.astype(out[name].dtype))
    for name, factor in factors.items():
        out[name] = (out[name] * factor).astype(out[name].dtype)
    return out
```

```python
import concourse.bass as bass
from concourse import mybir
from contextlib import ExitStack


P = 128
F32 = mybir.dt.float32
F32R = mybir.dt.float32r
U32 = mybir.dt.uint32
ALU = mybir.AluOpType
ACT = mybir.ActivationFunctionType
AX = mybir.AxisListType

IMAGES, CHANNELS, SIDE, PATCH = 64, 3, 224, 16
GRID = SIDE // PATCH
PLACES = GRID * GRID
D = 128
K_PATCH = CHANNELS * PATCH * PATCH
KT = K_PATCH // P
ROWS8 = P // PATCH
HEADS, DH = 8, 64
PAIRS = HEADS // 2
EXPERTS, FF, PARTS = 6, 341, 11
FT = -(-EXPERTS * FF // P)
FPAD = FT * P
EPS = 1e-5
MASKED = -1000000.0
TILES = PLACES * IMAGES // P
HALF_W = GRID // 2
CHUNKS = TILES // HALF_W
BODY = 2 * HALF_W
AHEAD = 3
BEHIND = 2
START = BEHIND + 1
TURNS = (TILES - AHEAD - START) // BODY
HALVES = 2
IPAIRS = IMAGES // 2
PT = 2 * PLACES
HP = PLACES // 2


class Tile:

    def __init__(self, turn, k):
        self.turn, self.k = turn, k

    def plus(self, d):
        return Tile(self.turn, self.k + d)

    def count(self, per, extra):
        return self.turn * (per * BODY) + (per * self.k + extra)

    def looped(self):
        return not isinstance(self.turn, int)

    def real(self):
        return self.looped() or 0 <= self.k < TILES


def until(eng, sem, value):
    if not isinstance(value, int) or value > 0:
        eng.wait_ge(sem, value)


def steps(eng, step):
    for n in range(-AHEAD, START):
        step(Tile(0, n))
    with eng.Fori(0, TURNS) as turn:
        for n in range(START, START + BODY):
            step(Tile(turn, n))
    for n in range(START + TURNS * BODY, TILES + BEHIND):
        step(Tile(0, n))


class Pair:

    def __init__(self, turn, k):
        self.turn, self.k = turn, k

    def plus(self, d):
        return Pair(self.turn, self.k + d)

    def count(self, per, extra):
        return self.turn * (2 * per) + (per * self.k + extra)

    def number(self):
        return self.k if isinstance(self.turn, int) else None

    def first(self):
        return self.number() == 0

    def last(self):
        return self.number() == IPAIRS - 1


def pairs(eng, pair):
    for k in range(2):
        pair(Pair(0, k))
    with eng.Fori(0, (IPAIRS - 4) // 2) as turn:
        for k in range(2, 4):
            pair(Pair(turn, k))
    for k in range(IPAIRS - 2, IPAIRS):
        pair(Pair(0, k))


def build(nc, x, tok_w, tok_b, wq, wkv, wo, router_w, w1, b1, w2, b2, part_w, out):
    h1_dram = nc.dram_tensor("h1_dram", (IMAGES, PLACES, D), F32, kind="Internal").ap()
    ctx = ExitStack()
    with ctx:
        def sb(name, shape, dt=F32, at=ctx):
            return at.enter_context(nc.sbuf_tensor(name, shape, dt))

        def sem(name):
            return ctx.enter_context(nc.semaphore(name))

        z2T = sb("z2T", [P, IMAGES, PLACES])
        w1_raw = sb("w1_raw", [P, FPAD])
        w2_raw = sb("w2_raw", [P, FT, D])
        ident = sb("ident", [P, P])
        b1_rows = sb("b1_rows", [FT, P])
        b1_col = sb("b1_col", [P, FT])
        b2_sb = sb("b2_sb", [EXPERTS, D])
        router_sb = sb("router_sb", [PARTS, D])
        routerT = sb("routerT", [P, PARTS])
        part_sb = sb("part_sb", [PARTS, EXPERTS])
        eps = sb("eps", [P, 1])

        one = ExitStack()
        xbuf = sb("xbuf", [P, 2, CHANNELS * PATCH, HALF_W * PATCH], at=one)
        patch = sb("patch", [P, 2, CHANNELS * PATCH, PATCH], at=one)
        tw_raw = sb("tw_raw", [P, K_PATCH], at=one)
        wq_raw = sb("wq_raw", [P, PAIRS, D], at=one)
        wk_raw = sb("wk_raw", [P, PAIRS, D], at=one)
        wv_raw = sb("wv_raw", [P, PAIRS, D], at=one)
        wo_raw = sb("wo_raw", [P, HEADS * DH], at=one)
        woT = sb("woT", [P, PAIRS, D], at=one)
        tok_bias = sb("tok_bias", [P, D], at=one)
        twT_hi = sb("twT_hi", [P, KT, D], F32R, at=one)
        twT_lo = sb("twT_lo", [P, KT, D], F32R, at=one)
        qk_hi = sb("qk_hi", [P, 2, PAIRS, D], F32R, at=one)
        qk_lo = sb("qk_lo", [P, 2, PAIRS, D], F32R, at=one)
        vo = sb("vo", [P, 2, PAIRS, D], at=one)
        mask = sb("mask", [P, HEADS, IMAGES], at=one)
        xT_hi = sb("xT_hi", [P, HALVES, KT // 2, P], F32R, at=one)
        xT_lo = sb("xT_lo", [P, HALVES, KT // 2, P], F32R, at=one)
        h0 = sb("h0", [P, HALF_W, D], at=one)
        z = sb("z", [P, 2, D], at=one)
        zT = sb("zT", [P, HALF_W, P], at=one)
        zT_hi = sb("zT_hi", [P, 2, P], F32R, at=one)
        zT_lo = sb("zT_lo", [P, 2, P], F32R, at=one)
        kq = sb("kq", [P, 2, HEADS, P], at=one)
        vw = sb("vw", [P, 2, 2, PAIRS, D], at=one)
        sm = sb("sm", [P, 2, HEADS, IMAGES], at=one)
        pe_ = sb("pe_", [P, 2, HEADS, IMAGES], at=one)
        pT = sb("pT", [P, PAIRS, P], at=one)
        h1 = sb("h1", [P, 2, D], at=one)
        z2 = sb("z2", [P, 2, D], at=one)
        smax = sb("smax", [P, 2, HEADS], at=one)
        ssum = sb("ssum", [P, 2, HEADS], at=one)
        sinv = sb("sinv", [P, 2, HEADS], at=one)
        stats = sb("stats", [P, 2, 6], at=one)
        moments = sb("moments", [P, 2, 2], at=one)
        lnv = sb("lnv", [P, 2, 1], at=one)
        guess = sb("guess", [P, 2, 1], at=one)
        newt = sb("newt", [P, 2, 2], at=one)
        rstd = sb("rstd", [P, 2, 1], at=one)
        one.close()

        two = ExitStack()
        w1_hi = sb("w1_hi", [P, FPAD], F32R, at=two)
        w1_lo = sb("w1_lo", [P, FPAD], F32R, at=two)
        w2_hi = sb("w2_hi", [P, FT, D], F32R, at=two)
        w2_lo = sb("w2_lo", [P, FT, D], F32R, at=two)
        onehot = sb("onehot", [EXPERTS, FPAD], at=two)
        places = sb("places", [IMAGES, PARTS], at=two)
        zsum = sb("zsum", [P, IMAGES], at=two)
        gate = sb("gate", [IMAGES, 8, 16], at=two)
        gate_idx = sb("gate_idx", [IMAGES, 8], U32, at=two)
        gateT = sb("gateT", [PARTS, IMAGES], at=two)
        ew_raw = sb("ew_raw", [EXPERTS, IMAGES], at=two)
        ew = sb("ew", [EXPERTS, IMAGES], at=two)
        ew_unit = sb("ew_unit", [P, FT, IMAGES], at=two)
        b2w = sb("b2w", [P, IMAGES], at=two)
        ewp = sb("ewp", [P, 2, FT, 2], at=two)
        b2p = sb("b2p", [P, 2, 2], at=two)
        zp_hi = sb("zp_hi", [P, 2, PT], F32R, at=two)
        zp_lo = sb("zp_lo", [P, 2, PT], F32R, at=two)
        g = sb("g", [P, 4, PT], at=two)
        gw_hi = sb("gw_hi", [P, 4, PT], F32R, at=two)
        gw_lo = sb("gw_lo", [P, 4, PT], F32R, at=two)
        yT = sb("yT", [P, 2, PT], at=two)
        h1_in = sb("h1_in", [HP, 2, 4, D], at=two)
        o_sb = sb("o_sb", [HP, 2, 4, D], at=two)
        two.close()

        bank = [ctx.enter_context(nc.psum_tensor(f"bank{i}", [P, 512], F32)) for i in range(8)]
        xT_ps = bank[0:2]
        wide = bank[2:4]
        s_ps, t_ps, y_ps, h_ps = bank[4:8]

        tw_in, bias_in, attn_w_in, mlp_w_in = sem("tw_in"), sem("bias_in"), sem("attn_w_in"), sem("mlp_w_in")
        x_in = [sem("x_in0"), sem("x_in1")]
        consts, zeroed, prep_pe, prep_ev, prep_hi = \
            sem("consts"), sem("zeroed"), sem("prep_pe"), sem("prep_ev"), sem("prep_hi")
        packed = sem("packed")
        xT_ready, xT_hi_done, xT_lo_done = sem("xT_ready"), sem("xT_hi_done"), sem("xT_lo_done")
        proj_ready, h0_done = sem("proj_ready"), sem("h0_done")
        ln_vec = [sem("ln1_vec"), sem("ln2_vec")]
        ln_act = [sem("ln1_act"), sem("ln2_act")]
        z_ready, zT_ready, zT_done, zT_hi_done, zT_lo_done = \
            sem("z_ready"), sem("zT_ready"), sem("zT_done"), sem("zT_hi_done"), sem("zT_lo_done")
        kq_ready, kq_done = sem("kq_ready"), sem("kq_done")
        vw_ready, vw_done = sem("vw_ready"), sem("vw_done")
        s_ready, masked, max_done, shifted, exp_done, sum_done, inv_done, p_ready = \
            sem("s_ready"), sem("masked"), sem("max_done"), sem("shifted"), sem("exp_done"), \
            sem("sum_done"), sem("inv_done"), sem("p_ready")
        pT_ready, pT_done, pv_ready, h1_done = sem("pT_ready"), sem("pT_done"), sem("pv_ready"), sem("h1_done")
        h1_saved = [sem("h1_saved0"), sem("h1_saved1")]
        z2_ready, z2T_ready, z2T_done = sem("z2_ready"), sem("z2T_ready"), sem("z2T_done")
        route_vec, route_pe, route_act, route_pool = \
            sem("route_vec"), sem("route_pe"), sem("route_act"), sem("route_pool")
        w_hi_done, w_lo_done = sem("w_hi_done"), sem("w_lo_done")
        zp_hi_done, zp_ready = sem("zp_hi_done"), sem("zp_ready")
        up_ready, gelu_done, gw_hi_done, gw_ready, down_done = \
            sem("up_ready"), sem("gelu_done"), sem("gw_hi_done"), sem("gw_ready"), sem("down_done")
        yT_done, o_ready, o_done = sem("yT_done"), sem("o_ready"), sem("o_done")
        h1_loaded = [sem("h1_loaded0"), sem("h1_loaded1")]
        o_saved = [sem("o_saved0"), sem("o_saved1")]

        block = ctx.enter_context(nc.Block())

        def load_x(eng, r, half):
            for a in range(2):
                src = x[:, :, bass.ds((2 * r + a) * PATCH, PATCH), half * HALF_W * PATCH:(half + 1) * HALF_W * PATCH]
                src = src.rearrange("b c y w -> b c y w")
                for c in range(CHANNELS):
                    eng.dma_start(xbuf[a * IMAGES:(a + 1) * IMAGES, half, c * PATCH:(c + 1) * PATCH, :],
                                  src[:, c, :, :]).then_inc(x_in[half], 16)
        X_DMAS = 2 * CHANNELS * 16

        @block.sync
        def _(sp):
            load_x(sp, 0, 0)
            load_x(sp, 0, 1)

            def save_h1(m):
                sp.wait_ge(h1_done, m.count(1, 1))
                r2 = m.k // GRID * 2
                w = m.k % GRID
                for a in range(2):
                    place = m.turn * (2 * GRID) + ((r2 + a) * GRID + w)
                    sp.dma_start(h1_dram[:, bass.ds(place, 1), :].rearrange("b o d -> b (o d)"),
                                 h1[a * IMAGES:(a + 1) * IMAGES, m.k % 2, :]).then_inc(h1_saved[m.k % 2], 16)

            def step(n):
                m = n.plus(AHEAD)
                if m.real() and m.k % HALF_W == HALF_W - 1 and (m.looped() or m.k + BODY < TILES):
                    sp.wait_ge(packed, m.count(1, 1))
                    load_x(sp, m.turn + (m.k // BODY + 1), m.k // HALF_W % 2)
                if n.plus(-1).real():
                    save_h1(n.plus(-1))

            steps(sp, step)
            for k in range(2):
                sp.wait_ge(h1_saved[k], 32 * TILES // 2)

            def load_h1(j):
                if j.number() not in (0, 1):
                    sp.wait_ge(o_done, j.count(1, -1))
                for b in range(2):
                    img = j.count(2, b)
                    sp.dma_start(h1_in[:, j.k % 2, 2 * b:2 * b + 2, :],
                                 h1_dram[bass.ds(img, 1), :, :].rearrange("o (p a) d -> (o p) a d", a=2)
                                 ).then_inc(h1_loaded[j.k % 2], 16)

            def save(j):
                sp.wait_ge(o_done, j.count(1, 1))
                for b in range(2):
                    img = j.count(2, b)
                    sp.dma_start(out[bass.ds(img, 1), :, :].rearrange("o (p a) d -> (o p) a d", a=2),
                                 o_sb[:, j.k % 2, 2 * b:2 * b + 2, :]).then_inc(o_saved[j.k % 2], 16)

            def pair(j):
                load_h1(j)
                if not j.first():
                    save(j.plus(-1))
                if j.last():
                    save(j)
            pairs(sp, pair)
            for k in range(2):
                sp.wait_ge(o_saved[k], 32 * IPAIRS // 2)

        @block.gpsimd
        def _(pool):
            pool.memset(ident[:, :], 0.0).then_inc(zeroed, 1)
            pool.memset(mask[:, :, :], 3.0e38).then_inc(zeroed, 1)
            pool.memset(eps[:, :], EPS).then_inc(consts, 1)
            pool.memset(b1_rows[:, :], 0.0).then_inc(zeroed, 1)
            pool.memset(w1_raw[:, EXPERTS * FF:FPAD], 0.0).then_inc(zeroed, 1)
            pool.memset(w2_raw[:, FT - 1, :], 0.0).then_inc(zeroed, 1)
            pool.wait_ge(zeroed, 5)
            pool.affine_select(out=ident[:, :], in_=ident[:, :], compare_op=ALU.not_equal, fill=1.0,
                               base=0, pattern=[[-1, P]], channel_multiplier=1).then_inc(consts, 1)
            for a in range(2):
                pool.wait_ge(consts, 2 + a)
                m = mask[a * IMAGES:(a + 1) * IMAGES, :, :]
                pool.affine_select(out=m, in_=m, compare_op=ALU.is_ge, fill=MASKED, base=0,
                                   pattern=[[0, HEADS], [-1, IMAGES]], channel_multiplier=1).then_inc(consts, 1)

            pool.wait_ge(consts, 4)

            def step(n):
                emb = n.plus(AHEAD)
                b = n.k % 2
                c, w = emb.k // HALF_W % 2, emb.k % HALF_W
                if emb.real():
                    if w == 0:
                        pool.wait_ge(x_in[c], emb.turn * X_DMAS + X_DMAS * (emb.k // BODY + 1))
                    until(pool, xT_ready, emb.count(2, -2))
                if n.real():
                    pool.wait_ge(max_done, n.count(1, 1))
                    pool.tensor_tensor(sm[:, b, :, :], sm[:, b, :, :],
                                       smax[:, b, :].unsqueeze(2).to_broadcast([P, HEADS, IMAGES]),
                                       ALU.subtract).then_inc(shifted, 1)
                if emb.real():
                    pool.tensor_copy(patch[:, emb.k % 2, :, :],
                                     xbuf[:, c, :, w * PATCH:(w + 1) * PATCH]).then_inc(packed, 1)
                if n.real():
                    pool.wait_ge(inv_done, n.count(1, 1))
                    pool.tensor_tensor(pe_[:, b, :, :], pe_[:, b, :, :],
                                       sinv[:, b, :].unsqueeze(2).to_broadcast([P, HEADS, IMAGES]),
                                       ALU.mult).then_inc(p_ready, 1)
            steps(pool, step)

            pool.wait_ge(z2T_done, TILES)
            for k in range(2):
                pool.wait_ge(h1_saved[k], 32 * TILES // 2)
            pool.memset(onehot[:, :], 1.0).then_inc(route_pool, 1)
            pool.iota(places[:, :], pattern=[[1, PARTS]], base=0, channel_multiplier=0,
                      allow_small_or_imprecise_dtypes=True).then_inc(route_pool, 1)
            pool.wait_ge(route_pool, 2)
            pool.affine_select(out=onehot[:, :], in_=onehot[:, :], compare_op=ALU.is_ge, fill=0.0, base=0,
                               pattern=[[1, FPAD]], channel_multiplier=-FF).then_inc(route_pool, 1)
            pool.wait_ge(route_pool, 3)
            pool.affine_select(out=onehot[:, :], in_=onehot[:, :], compare_op=ALU.is_ge, fill=0.0, base=FF - 1,
                               pattern=[[-1, FPAD]], channel_multiplier=FF).then_inc(route_pool, 1)

        @block.scalar
        def _(act):
            act.dma_start(tw_raw[:, :], tok_w).then_inc(tw_in, 16)
            act.dma_start(tok_bias[:, :], tok_b.partition_broadcast(P)).then_inc(bias_in, 16)
            for dst, src in ((wq_raw, wq), (wk_raw, wkv[0:HEADS * DH, :]), (wv_raw, wkv[HEADS * DH:2 * HEADS * DH, :])):
                act.dma_start(dst[:, :, :], src.rearrange("(t p) j -> p t j", p=P)).then_inc(attn_w_in, 16)
            act.dma_start(wo_raw[:, :], wo).then_inc(attn_w_in, 16)
            act.wait_ge(zeroed, 5)
            full = (FT - 1) * P
            rest = EXPERTS * FF - full
            act.dma_start(w1_raw[:, 0:EXPERTS * FF].rearrange("p (e f) -> p e f", e=EXPERTS),
                          w1.rearrange("e d f -> d e f")).then_inc(mlp_w_in, 16)
            w2_rows = w2.rearrange("e f d -> (e f) d")
            act.dma_start(w2_raw[:, 0:FT - 1, :], w2_rows[0:full, :].rearrange("(t p) d -> p t d", p=P)).then_inc(mlp_w_in, 16)
            act.dma_start(w2_raw[0:rest, FT - 1, :], w2_rows[full:full + rest, :]).then_inc(mlp_w_in, 16)
            b1_flat = b1.rearrange("e f -> (e f)")
            act.dma_start(b1_rows[0:FT - 1, :], b1_flat[0:full].rearrange("(t p) -> t p", p=P)).then_inc(mlp_w_in, 16)
            act.dma_start(b1_rows[FT - 1:FT, 0:rest], b1_flat[full:full + rest].rearrange("(o p) -> o p", o=1)).then_inc(mlp_w_in, 16)
            act.dma_start(b2_sb[:, :], b2).then_inc(mlp_w_in, 16)
            act.dma_start(router_sb[:, :], router_w).then_inc(mlp_w_in, 16)
            act.dma_start(part_sb[:, :], part_w).then_inc(mlp_w_in, 16)

            nc.scalar.preload_act_table_set("natural_log_exp_and_others")
            for i in range(2):
                act.wait_ge(prep_pe, i + 1)
                act.activation(twT_hi[:, 3 * i:3 * i + 3, :], bank[i][:, 0:3 * P].rearrange("p (k e) -> p k e", e=D),
                               ACT.Copy).then_inc(prep_hi, 1)
            for q in range(2):
                act.wait_ge(prep_pe, 4 + q)
                act.activation(qk_hi[:, q, :, :], bank[4 + q][:, :].rearrange("p (k e) -> p k e", e=D),
                               ACT.Copy, scale=DH ** -0.5).then_inc(prep_hi, 1)

            def log_exp(m, which):
                act.wait_ge(ln_vec[which], m.count(5, 2))
                act.activation(lnv[:, which, :], moments[:, which, 1:2], ACT.Ln, bias=eps[:, 0:1]).then_inc(ln_act[which], 1)
                act.wait_ge(ln_act[which], m.count(2, 1))
                act.activation(guess[:, which, :], lnv[:, which, :], ACT.Exp, scale=-0.5).then_inc(ln_act[which], 1)

            def split_x(m, h):
                act.wait_ge(xT_ready, m.count(2, h + 1))
                act.activation(xT_hi[:, h, :, :], xT_ps[h][:, 0:3 * P].rearrange("p (k t) -> p k t", t=P),
                               ACT.Copy).then_inc(xT_hi_done, 1)

            def take_vw(n, a):
                act.wait_ge(vw_ready, n.count(2, a + 1))
                if a == 0:
                    until(act, pv_ready, n.count(1, -1))
                act.activation(vw[:, n.k % 2, a, :, :], wide[a][:, :].rearrange("p (t f) -> p t f", f=D),
                               ACT.Copy).then_inc(vw_done, 1)

            def take_kq(m, a):
                act.wait_ge(kq_ready, m.count(2, a + 1))
                act.activation(kq[:, m.k % 2, 4 * a:4 * a + 4, :], wide[a][:, :].rearrange("p (h t) -> p h t", t=P),
                               ACT.Copy).then_inc(kq_done, 1)

            act.wait_ge(consts, 1)

            def step(n):
                emb, nrm, key, prev, last = n.plus(AHEAD), n.plus(2), n.plus(1), n.plus(-1), n.plus(-BEHIND)
                if last.real():
                    log_exp(last, 1)
                if emb.real():
                    split_x(emb, 0)
                if nrm.real():
                    act.wait_ge(zT_ready, nrm.count(1, 1))
                    act.activation(zT[:, nrm.k % HALF_W, :], t_ps[:, 0:P], ACT.Copy).then_inc(zT_done, 1)
                    act.activation(zT_hi[:, nrm.k % 2, :], t_ps[:, 0:P], ACT.Copy).then_inc(zT_hi_done, 1)
                if emb.real():
                    split_x(emb, 1)
                if n.real():
                    take_vw(n, 0)
                    act.wait_ge(shifted, n.count(1, 1))
                    until(act, pT_ready, n.count(1, -1))
                    act.activation(pe_[:, n.k % 2, :, :], sm[:, n.k % 2, :, :], ACT.Exp).then_inc(exp_done, 1)
                    take_vw(n, 1)
                if prev.real():
                    act.wait_ge(pT_ready, prev.count(1, 1))
                    act.activation(pT[:, :, :], t_ps[:, :].rearrange("p (t q) -> p t q", q=P), ACT.Copy).then_inc(pT_done, 1)
                if key.real():
                    until(act, s_ready, key.count(1, -1))
                    take_kq(key, 0)
                if emb.real():
                    log_exp(emb, 0)
                if key.real():
                    take_kq(key, 1)
                if last.real():
                    act.wait_ge(z2T_ready, last.count(1, 1))
                    w0 = last.turn * (2 * GRID) + (last.k // GRID * 2 * GRID + last.k % GRID)
                    for a in range(2):
                        act.activation(z2T[:, :, bass.ds(w0 + a * GRID, 1)].rearrange("p b o -> p (b o)"),
                                       h_ps[:, a * IMAGES:(a + 1) * IMAGES], ACT.Copy).then_inc(z2T_done, 1)
            steps(act, step)

            act.wait_ge(mlp_w_in, 8 * 16)
            act.wait_ge(p_ready, TILES)
            act.wait_ge(h1_saved[0], 32 * TILES // 2)
            act.wait_ge(h1_saved[1], 32 * TILES // 2)
            act.activation(w1_hi[:, :], w1_raw[:, :], ACT.Copy).then_inc(w_hi_done, 1)
            act.activation(w2_hi[:, :, :], w2_raw[:, :, :], ACT.Copy).then_inc(w_hi_done, 1)
            act.wait_ge(route_vec, 3)
            act.activation(gate[:, 1, 0:PARTS], gate[:, 0, 0:PARTS], ACT.Exp, bias=gate[:, 2, 8:9]).then_inc(route_act, 1)

            def gelu(j, t):
                act.wait_ge(up_ready, j.count(FT, t + 1))
                if not (j.first() and t < 4):
                    act.wait_ge(gw_ready, j.count(FT, t - 3))
                act.activation(g[:, t % 4, :], bank[t % 4][:, 0:PT], ACT.Gelu,
                               bias=b1_col[:, t:t + 1]).then_inc(gelu_done, 1)

            def take_y(j):
                act.wait_ge(down_done, j.count(FT, FT))
                if not j.first():
                    act.wait_ge(o_ready, j.count(1, 0))
                for b in range(2):
                    act.activation(yT[:, j.k % 2, b * PLACES:(b + 1) * PLACES],
                                   bank[4 + j.k % 2][:, b * PLACES:(b + 1) * PLACES], ACT.Identity,
                                   bias=b2p[:, j.k % 2, b:b + 1]).then_inc(yT_done, 1)

            act.wait_ge(route_vec, 19)

            def pair(j):
                for t in range(FT):
                    gelu(j, t)
                    if t == 2 and not j.first():
                        take_y(j.plus(-1))
                if j.last():
                    take_y(j)
            pairs(act, pair)

        @block.tensor
        def _(pe):
            def mm3(o, a_hi, a_lo, b_hi, b_lo, start, stop):
                pe.matmul(o, a_hi, b_hi, start=start, stop=False)
                pe.matmul(o, a_lo, b_hi, start=False, stop=False)
                return pe.matmul(o, a_hi, b_lo, start=False, stop=stop)

            pe.wait_ge(consts, 4)
            pe.wait_ge(tw_in, 16)
            for i in range(2):
                for k in range(3):
                    mm = pe.transpose(bank[i][:, k * P:(k + 1) * P], tw_raw[:, (3 * i + k) * P:(3 * i + k + 1) * P], ident[:, :])
                mm.then_inc(prep_pe, 1)
            pe.wait_ge(attn_w_in, 4 * 16)
            for t in range(PAIRS):
                mm = pe.transpose(bank[2][:, t * P:(t + 1) * P], wo_raw[:, t * P:(t + 1) * P], ident[:, :])
            mm.then_inc(prep_pe, 1)
            for q in range(2):
                for t in range(PAIRS):
                    r = slice(q * DH, (q + 1) * DH)
                    mm = pe.matmul(bank[4 + q][:, t * P:(t + 1) * P], wk_raw[r, t, :], wq_raw[r, t, :], start=True, stop=True)
                mm.then_inc(prep_pe, 1)
            pe.wait_ge(prep_ev, 3)
            for q in range(2):
                for t in range(PAIRS):
                    r = slice(q * DH, (q + 1) * DH)
                    mm = pe.matmul(bank[6 + q][:, t * P:(t + 1) * P], wv_raw[r, t, :], woT[r, t, :], start=True, stop=True)
                mm.then_inc(prep_pe, 1)
            pe.wait_ge(mlp_w_in, 8 * 16)
            pe.transpose(bank[3][:, 0:FT], b1_rows[:, :], ident[0:FT, 0:FT])
            pe.transpose(bank[3][:, 64:64 + PARTS], router_sb[:, :], ident[0:PARTS, 0:PARTS]).then_inc(prep_pe, 1)
            pe.wait_ge(prep_ev, 9)

            def turn_x(m, h):
                if h == 0:
                    pe.wait_ge(packed, m.count(1, 1))
                until(pe, xT_lo_done, m.count(2, h - 1))
                for k in range(3):
                    row = (3 * h + k) * ROWS8
                    mm = pe.transpose(xT_ps[h][:, k * P:(k + 1) * P],
                                      patch[:, m.k % 2, row:row + ROWS8, :].rearrange("p r c -> p (r c)"), ident[:, :])
                mm.then_inc(xT_ready, 1)

            def project(m):
                pe.wait_ge(xT_lo_done, m.count(2, 2))
                until(pe, z2T_done, m.count(2, -2 * 5))
                for k in range(KT):
                    h, kk = k // 3, k % 3
                    mm = mm3(h_ps[:, 0:D], xT_hi[:, h, kk, :], xT_lo[:, h, kk, :], twT_hi[:, k, :], twT_lo[:, k, :],
                             k == 0, k == KT - 1)
                mm.then_inc(proj_ready, 1)

            def turn_z(m):
                pe.wait_ge(z_ready, m.count(1, 1))
                until(pe, pT_done, m.count(1, -3))
                pe.transpose(t_ps[:, 0:P], z[:, m.k % 2, :], ident[:, :]).then_inc(zT_ready, 1)

            def keys(m, a):
                if a == 0:
                    pe.wait_ge(zT_lo_done, m.count(1, 1))
                if n_real_before(m):
                    until(pe, vw_done, m.count(2, -1 + a))
                for h in range(4):
                    t, q = (4 * a + h) // 2, h % 2
                    mm = mm3(wide[a][:, h * P:(h + 1) * P], qk_hi[:, q, t, :], qk_lo[:, q, t, :],
                             zT_hi[:, m.k % 2, :], zT_lo[:, m.k % 2, :], True, True)
                mm.then_inc(kq_ready, 1)

            def n_real_before(m):
                return m.looped() or m.k >= 1

            def values(n, a):
                pe.wait_ge(kq_done, n.count(2, a + 1))
                lhs = zT[:, n.k % HALF_W, a * IMAGES:(a + 1) * IMAGES]
                for q in range(2):
                    mm = pe.matmul(wide[a][q * IMAGES:(q + 1) * IMAGES, :], lhs, vo[:, q, :, :], start=True, stop=True)
                mm.then_inc(vw_ready, 1)

            def scores(n):
                pe.wait_ge(kq_done, n.count(2, 2))
                until(pe, masked, n.count(1, 0))
                for a in range(2):
                    t = slice(a * IMAGES, (a + 1) * IMAGES)
                    mm = pe.matmul(s_ps[t, :], zT[:, n.k % HALF_W, t], kq[:, n.k % 2, :, t], start=True, stop=True)
                mm.then_inc(s_ready, 1)

            def turn_p(m):
                pe.wait_ge(p_ready, m.count(1, 1))
                pe.wait_ge(zT_lo_done, m.count(1, 4) if m.looped() else min(m.k + 4, TILES))
                for t in range(PAIRS):
                    mm = pe.transpose(t_ps[:, t * P:(t + 1) * P], pe_[:, m.k % 2, 2 * t:2 * t + 2, :].rearrange("p h k -> p (h k)"), ident[:, :])
                mm.then_inc(pT_ready, 1)

            def mix(m):
                pe.wait_ge(pT_done, m.count(1, 1))
                pe.wait_ge(vw_done, m.count(2, 2))
                until(pe, h1_done, m.count(1, 0))
                for t in range(PAIRS):
                    for a in range(2):
                        s = slice(a * IMAGES, (a + 1) * IMAGES)
                        mm = pe.matmul(y_ps[s, 0:D], pT[:, t, s], vw[:, m.k % 2, a, t, :],
                                       start=(t == 0), stop=(t == PAIRS - 1))
                mm.then_inc(pv_ready, 1)

            def turn_z2(m):
                pe.wait_ge(z2_ready, m.count(1, 1))
                h0_seen = m.count(1, 6) if m.looped() else min(m.k + 6, TILES)
                pe.wait_ge(h0_done, h0_seen)
                pe.transpose(h_ps[:, 0:P], z2[:, m.k % 2, :], ident[:, :]).then_inc(z2T_ready, 1)

            def step(n):
                emb, nrm, key, prev, last = n.plus(AHEAD), n.plus(2), n.plus(1), n.plus(-1), n.plus(-BEHIND)
                if n.real():
                    scores(n)
                if emb.real():
                    turn_x(emb, 0)
                if nrm.real():
                    turn_z(nrm)
                if n.real():
                    values(n, 0)
                if emb.real():
                    turn_x(emb, 1)
                if n.real():
                    values(n, 1)
                if prev.real():
                    turn_p(prev)
                if key.real():
                    keys(key, 0)
                if emb.real():
                    project(emb)
                if key.real():
                    keys(key, 1)
                if prev.real():
                    mix(prev)
                if last.real():
                    turn_z2(last)
            steps(pe, step)

            pe.wait_ge(route_vec, 1)
            pe.wait_ge(z2T_done, 2 * TILES)
            pe.matmul(bank[6][0:IMAGES, 0:PARTS], zsum[:, :], routerT[:, :], start=True, stop=True).then_inc(route_pe, 1)
            pe.wait_ge(route_vec, 13)
            pe.transpose(bank[6][0:PARTS, 0:IMAGES], gate[:, 7, 0:PARTS], ident[0:IMAGES, 0:IMAGES]).then_inc(route_pe, 1)
            pe.wait_ge(route_vec, 14)
            pe.matmul(bank[6][0:EXPERTS, 0:IMAGES], part_sb[:, :], gateT[:, :], start=True, stop=True).then_inc(route_pe, 1)
            pe.wait_ge(route_vec, 16)
            pe.wait_ge(route_pool, 4)
            for t in range(FT):
                mm = pe.matmul(bank[4 + t // 8][:, t % 8 * IMAGES:(t % 8 + 1) * IMAGES], onehot[:, t * P:(t + 1) * P],
                               ew[:, :], start=True, stop=True)
            pe.matmul(bank[6][:, 0:IMAGES], b2_sb[:, :], ew[:, :], start=True, stop=True).then_inc(route_pe, 1)
            pe.wait_ge(w_lo_done, 2)

            def up(j, t):
                if t == 0:
                    pe.wait_ge(zp_ready, j.count(1, 1))
                if not (j.first() and t < 4):
                    pe.wait_ge(gelu_done, j.count(FT, t - 3))
                f = slice(t * P, (t + 1) * P)
                mm3(bank[t % 4][:, 0:PT], w1_hi[:, f], w1_lo[:, f], zp_hi[:, j.k % 2, :], zp_lo[:, j.k % 2, :],
                    True, True).then_inc(up_ready, 1)

            def down(j, t):
                pe.wait_ge(gw_ready, j.count(FT, t + 1))
                if t == 0 and j.number() not in (0, 1):
                    pe.wait_ge(yT_done, j.count(2, -2))
                mm = mm3(bank[4 + j.k % 2][:, 0:PT], w2_hi[:, t, :], w2_lo[:, t, :], gw_hi[:, t % 4, :],
                         gw_lo[:, t % 4, :], t == 0, t == FT - 1)
                mm.then_inc(down_done, 1)
                return mm

            def turn_y(j):
                pe.wait_ge(yT_done, j.count(2, 2))
                if not j.first():
                    pe.wait_ge(o_done, j.count(1, 0))
                for b in range(2):
                    for a in range(2):
                        c = 2 * b + a
                        mm = pe.transpose(bank[6][0:HP, c * D:(c + 1) * D],
                                          yT[:, j.k % 2, b * PLACES + a:(b + 1) * PLACES:2], ident[:, :])
                mm.then_inc(o_ready, 1)

            pe.wait_ge(route_vec, 19)
            lead = 2
            for t in range(lead):
                up(Pair(0, 0), t)

            def pair(j):
                for t in range(FT):
                    if t + lead < FT:
                        up(j, t + lead)
                    elif not j.last():
                        up(j.plus(1), t + lead - FT)
                    down(j, t)
                    if t == 5 and not j.first():
                        turn_y(j.plus(-1))
                if j.last():
                    turn_y(j)
            pairs(pe, pair)

        @block.vector
        def _(dve):
            for i in range(2):
                dve.wait_ge(prep_hi, i + 1)
                dve.tensor_tensor(twT_lo[:, 3 * i:3 * i + 3, :], bank[i][:, 0:3 * P].rearrange("p (k e) -> p k e", e=D),
                                  twT_hi[:, 3 * i:3 * i + 3, :].bitcast(F32), ALU.subtract).then_inc(prep_ev, 1)
            dve.wait_ge(prep_pe, 3)
            dve.tensor_copy(woT[:, :, :], bank[2][:, :].rearrange("p (t f) -> p t f", f=D)).then_inc(prep_ev, 1)
            for q in range(2):
                dve.wait_ge(prep_hi, 3 + q)
                dve.scalar_tensor_tensor(out=qk_lo[:, q, :, :], in0=bank[4 + q][:, :].rearrange("p (k e) -> p k e", e=D),
                                         scalar=DH ** -0.5, in1=qk_hi[:, q, :, :].bitcast(F32), op0=ALU.mult,
                                         op1=ALU.subtract).then_inc(prep_ev, 1)
            for q in range(2):
                dve.wait_ge(prep_pe, 6 + q)
                dve.tensor_copy(vo[:, q, :, :], bank[6 + q][:, :].rearrange("p (t f) -> p t f", f=D)).then_inc(prep_ev, 1)
            dve.wait_ge(prep_pe, 8)
            dve.tensor_copy(b1_col[:, :], bank[3][:, 0:FT]).then_inc(prep_ev, 1)
            dve.tensor_copy(routerT[:, :], bank[3][:, 64:64 + PARTS]).then_inc(prep_ev, 1)
            dve.wait_ge(bias_in, 16)
            dve.wait_ge(consts, 4)

            def stats_of(which, src):
                dve.bn_stats(stats[:, which, :], src).then_inc(ln_vec[which], 1)

            def moments_of(which):
                dve.bn_aggr(moments[:, which, :], stats[:, which, :]).then_inc(ln_vec[which], 1)

            def norm_apply(m, which, src, dst, done):
                y = guess[:, which, 0:1]
                dve.wait_ge(ln_act[which], m.count(2, 2))
                dve.tensor_scalar(newt[:, which, 0:1], moments[:, which, 1:2], EPS, y, ALU.add, ALU.mult).then_inc(ln_vec[which], 1)
                dve.wait_ge(ln_vec[which], m.count(5, 3))
                dve.tensor_scalar(newt[:, which, 1:2], newt[:, which, 0:1], y, -0.5, ALU.mult, ALU.mult).then_inc(ln_vec[which], 1)
                dve.wait_ge(ln_vec[which], m.count(5, 4))
                dve.tensor_scalar(rstd[:, which, :], newt[:, which, 1:2], 1.5, y, ALU.add, ALU.mult).then_inc(ln_vec[which], 1)
                dve.wait_ge(ln_vec[which], m.count(5, 5))
                dve.tensor_scalar(dst, src, moments[:, which, 0:1], rstd[:, which, 0:1], ALU.subtract, ALU.mult).then_inc(done, 1)

            def split_x(m, h):
                dve.wait_ge(xT_hi_done, m.count(2, h + 1))
                dve.tensor_tensor(xT_lo[:, h, :, :], xT_ps[h][:, 0:3 * P].rearrange("p (k t) -> p k t", t=P),
                                  xT_hi[:, h, :, :].bitcast(F32), ALU.subtract).then_inc(xT_lo_done, 1)

            def step(n):
                emb, nrm, last = n.plus(AHEAD), n.plus(2), n.plus(-BEHIND)
                b = n.k % 2
                if last.real():
                    dve.wait_ge(pv_ready, last.count(1, 1))
                    k = last.k // 2
                    until(dve, h1_saved[last.k % 2], last.turn * (16 * BODY) + 32 * k)
                    dve.tensor_tensor(h1[:, last.k % 2, :], y_ps[:, 0:D], h0[:, last.k % HALF_W, :], ALU.add).then_inc(h1_done, 1)
                    dve.wait_ge(h1_done, last.count(1, 1))
                    stats_of(1, h1[:, last.k % 2, :])
                    until(dve, ln_vec[1], last.count(5, 1))
                if n.real():
                    dve.wait_ge(s_ready, n.count(1, 1))
                    until(dve, exp_done, n.count(1, -1))
                    dve.tensor_tensor(sm[:, b, :, :], s_ps[:, :].rearrange("p (h k) -> p h k", k=IMAGES),
                                      mask[:, :, :], ALU.min).then_inc(masked, 1)
                if last.real():
                    moments_of(1)
                if n.real():
                    dve.wait_ge(masked, n.count(1, 1))
                    dve.tensor_reduce(smax[:, b, :], sm[:, b, :, :], AX.X, ALU.max).then_inc(max_done, 1)
                if emb.real():
                    split_x(emb, 0)
                if nrm.real():
                    dve.wait_ge(zT_hi_done, nrm.count(1, 1))
                    dve.tensor_tensor(zT_lo[:, nrm.k % 2, :], t_ps[:, 0:P], zT_hi[:, nrm.k % 2, :].bitcast(F32),
                                      ALU.subtract).then_inc(zT_lo_done, 1)
                if last.real():
                    norm_apply(last, 1, h1[:, last.k % 2, :], z2[:, last.k % 2, :], z2_ready)
                if emb.real():
                    split_x(emb, 1)
                if n.real():
                    dve.wait_ge(exp_done, n.count(1, 1))
                    dve.tensor_reduce(ssum[:, b, :], pe_[:, b, :, :], AX.X, ALU.add).then_inc(sum_done, 1)
                if emb.real():
                    dve.wait_ge(proj_ready, emb.count(1, 1))
                    dve.tensor_tensor(h0[:, emb.k % HALF_W, :], h_ps[:, 0:D], tok_bias[:, :], ALU.add).then_inc(h0_done, 1)
                    dve.wait_ge(h0_done, emb.count(1, 1))
                    stats_of(0, h0[:, emb.k % HALF_W, :])
                    until(dve, ln_vec[0], emb.count(5, 1))
                if n.real():
                    dve.wait_ge(sum_done, n.count(1, 1))
                    dve.reciprocal(sinv[:, b, :], ssum[:, b, :]).then_inc(inv_done, 1)
                if emb.real():
                    moments_of(0)
                    norm_apply(emb, 0, h0[:, emb.k % HALF_W, :], z[:, emb.k % 2, :], z_ready)
            steps(dve, step)

            rv = [0]

            def link(ins):
                rv[0] += 1
                ins.then_inc(route_vec, 1)

            dve.wait_ge(z2T_done, 2 * TILES)
            dve.wait_ge(p_ready, TILES)
            dve.wait_ge(h1_saved[0], 32 * TILES // 2)
            dve.wait_ge(h1_saved[1], 32 * TILES // 2)
            link(dve.tensor_reduce(zsum[:, :], z2T[:, :, :], AX.X, ALU.add))
            dve.wait_ge(w_hi_done, 1)
            dve.tensor_tensor(w1_lo[:, :], w1_raw[:, :], w1_hi[:, :].bitcast(F32), ALU.subtract).then_inc(w_lo_done, 1)
            dve.wait_ge(w_hi_done, 2)
            dve.tensor_tensor(w2_lo[:, :, :], w2_raw[:, :, :], w2_hi[:, :, :].bitcast(F32), ALU.subtract).then_inc(w_lo_done, 1)
            dve.wait_ge(route_pe, 1)
            link(dve.tensor_scalar(gate[:, 0, 0:PARTS], bank[6][0:IMAGES, 0:PARTS], 1.0 / PLACES, None, ALU.mult))
            dve.wait_ge(route_vec, 2)
            link(dve.tensor_reduce(gate[:, 2, 8:9], gate[:, 0, 0:PARTS], AX.X, ALU.max, negate=True))
            dve.wait_ge(route_act, 1)
            link(dve.tensor_reduce(gate[:, 2, 9:10], gate[:, 1, 0:PARTS], AX.X, ALU.add))
            dve.wait_ge(route_vec, 4)
            link(dve.reciprocal(gate[:, 2, 10:11], gate[:, 2, 9:10]))
            dve.wait_ge(route_vec, 5)
            link(dve.tensor_scalar(gate[:, 3, 0:PARTS], gate[:, 1, 0:PARTS], gate[:, 2, 10:11], None, ALU.mult))
            dve.wait_ge(route_vec, 6)
            link(dve.max(gate[:, 4, 0:8], gate[:, 3, 0:PARTS]))
            dve.wait_ge(route_vec, 7)
            link(dve.max_index(gate_idx[:, :], gate[:, 4, 0:8], gate[:, 3, 0:PARTS]))
            link(dve.tensor_tensor(gate[:, 2, 11:12], gate[:, 4, 0:1], gate[:, 4, 1:2], ALU.add))
            dve.wait_ge(route_vec, 9)
            link(dve.reciprocal(gate[:, 2, 12:13], gate[:, 2, 11:12]))
            link(dve.tensor_copy(gate[:, 2, 14:16], gate_idx[:, 0:2]))
            dve.wait_ge(route_vec, 11)
            dve.wait_ge(route_pool, 2)
            link(dve.tensor_scalar(gate[:, 5, 0:PARTS], places[:, :], gate[:, 2, 14:15], gate[:, 4, 0:1], ALU.is_equal, ALU.mult))
            dve.tensor_scalar(gate[:, 6, 0:PARTS], places[:, :], gate[:, 2, 15:16], gate[:, 4, 1:2],
                              ALU.is_equal, ALU.mult).then_inc(w_lo_done, 1)
            dve.wait_ge(route_vec, 12)
            dve.wait_ge(w_lo_done, 3)
            dve.tensor_tensor(gate[:, 7, 0:PARTS], gate[:, 5, 0:PARTS], gate[:, 6, 0:PARTS], ALU.add).then_inc(w_lo_done, 1)
            dve.wait_ge(w_lo_done, 4)
            link(dve.tensor_scalar(gate[:, 7, 0:PARTS], gate[:, 7, 0:PARTS], gate[:, 2, 12:13], None, ALU.mult))
            dve.wait_ge(route_pe, 2)
            link(dve.tensor_copy(gateT[:, :], bank[6][0:PARTS, 0:IMAGES]))
            dve.wait_ge(route_pe, 3)
            link(dve.tensor_copy(ew_raw[:, :], bank[6][0:EXPERTS, 0:IMAGES]))
            dve.wait_ge(route_vec, 15)
            link(dve.scalar_tensor_tensor(out=ew[:, :], in0=ew_raw[:, :], scalar=1e-6, in1=ew_raw[:, :],
                                          op0=ALU.is_gt, op1=ALU.mult))
            dve.wait_ge(route_pe, 4)
            for i in range(2):
                link(dve.tensor_copy(ew_unit[:, 8 * i:8 * i + 8, :],
                                     bank[4 + i][:, :].rearrange("p (t b) -> p t b", b=IMAGES)))
            link(dve.tensor_copy(b2w[:, :], bank[6][:, 0:IMAGES]))
            dve.wait_ge(route_vec, 19)

            def split_z(j):
                img = j.count(2, 0)
                src = z2T[:, bass.ds(img, 2), :].rearrange("p b t -> p (b t)")
                b = j.k % 2
                dve.tensor_copy(ewp[:, b, :, :], ew_unit[:, :, bass.ds(img, 2)])
                dve.tensor_copy(b2p[:, b, :], b2w[:, bass.ds(img, 2)])
                dve.tensor_copy(zp_hi[:, b, :], src).then_inc(zp_hi_done, 1)
                dve.wait_ge(zp_hi_done, j.count(1, 1))
                dve.tensor_tensor(zp_lo[:, b, :], src, zp_hi[:, b, :].bitcast(F32), ALU.subtract).then_inc(zp_ready, 1)

            def weigh(j, t):
                dve.wait_ge(gelu_done, j.count(FT, t + 1))
                if not (j.first() and t < 4):
                    dve.wait_ge(down_done, j.count(FT, t - 3))
                if t == 0:
                    dve.wait_ge(zp_ready, j.count(1, 1))
                for b in range(2):
                    s = slice(b * PLACES, (b + 1) * PLACES)
                    hi = dve.tensor_scalar(gw_hi[:, t % 4, s], g[:, t % 4, s], ewp[:, j.k % 2, t, b:b + 1], None, ALU.mult)
                hi.then_inc(gw_hi_done, 1)
                dve.wait_ge(gw_hi_done, j.count(FT, t + 1))
                for b in range(2):
                    s = slice(b * PLACES, (b + 1) * PLACES)
                    lo = dve.scalar_tensor_tensor(out=gw_lo[:, t % 4, s], in0=g[:, t % 4, s],
                                                  scalar=ewp[:, j.k % 2, t, b:b + 1],
                                                  in1=gw_hi[:, t % 4, s].bitcast(F32), op0=ALU.mult, op1=ALU.subtract)
                lo.then_inc(gw_ready, 1)

            def add_h1(j):
                dve.wait_ge(o_ready, j.count(1, 1))
                k = j.k // 2
                dve.wait_ge(h1_loaded[j.k % 2], j.turn * 32 + 32 * (k + 1))
                until(dve, o_saved[j.k % 2], j.turn * 32 + 32 * k)
                dve.tensor_tensor(o_sb[:, j.k % 2, :, :], bank[6][0:HP, :].rearrange("p (c d) -> p c d", d=D),
                                  h1_in[:, j.k % 2, :, :], ALU.add).then_inc(o_done, 1)

            split_z(Pair(0, 0))

            def pair(j):
                for t in range(FT):
                    weigh(j, t)
                    if t == 5 and not j.last():
                        split_z(j.plus(1))
                    if t == 7 and not j.first():
                        add_h1(j.plus(-1))
                if j.last():
                    add_h1(j)
            pairs(dve, pair)


_INS = ['x', 'L0_tok_w', 'L0_tok_b', 'L0_attn_Wq', 'L0_attn_Wkv', 'L0_attn_Wo', 'L0_ffn_router_w', 'L0_ffn_W1',
        'L0_ffn_b1', 'L0_ffn_W2', 'L0_ffn_b2']
_PARTITIONS = [(6,), (5, 1), (4, 2), (4, 1, 1), (3, 3), (3, 2, 1), (3, 1, 1, 1), (2, 2, 2), (2, 2, 1, 1),
               (2, 1, 1, 1, 1), (1, 1, 1, 1, 1, 1)]


def kernel(**inputs):
    import numpy as _np
    import concourse.bacc as _bacc
    from concourse import mybir as _mybir
    from concourse.bass_utils import run_bass_kernel_spmd as _run

    nc = _bacc.Bacc("TRN2", target_bir_lowering=False, num_devices=1)
    arrays, args = {}, []
    for name in _INS:
        a = _np.ascontiguousarray(inputs[name])
        arrays[f"in_{name}"] = a
        args.append(nc.dram_tensor(f"in_{name}", a.shape, _mybir.dt.from_np(a.dtype), kind="ExternalInput").ap())
    table = _np.zeros((PARTS, EXPERTS), dtype=_np.float32)
    for i, parts in enumerate(_PARTITIONS):
        for e, n in enumerate(parts):
            table[i, e] = n / 6
    arrays["in_part_w"] = table
    args.append(nc.dram_tensor("in_part_w", table.shape, F32, kind="ExternalInput").ap())
    out = nc.dram_tensor("out_0", (IMAGES, PLACES, D), F32, kind="ExternalOutput").ap()
    build(nc, *args, out)
    r = _run(nc, [arrays], core_ids=[0])
    return r.results[0]["out_0"]
```

```python
import concourse.bass as bass
from concourse import mybir
from contextlib import ExitStack


P = 128
F32 = mybir.dt.float32
F32R = mybir.dt.float32r
U32 = mybir.dt.uint32
I32 = mybir.dt.int32
ALU = mybir.AluOpType
ACT = mybir.ActivationFunctionType
AX = mybir.AxisListType

IMAGES, CHANNELS, SIDE, PATCH = 64, 3, 224, 16
GRID = SIDE // PATCH
PLACES = GRID * GRID
D = 128
K_PATCH = CHANNELS * PATCH * PATCH
KT = K_PATCH // P
ROWS8 = P // PATCH
HEADS, DH = 8, 64
PAIRS = HEADS // 2
EXPERTS, FF, PARTS = 6, 341, 11
FT = -(-EXPERTS * FF // P)
FPAD = FT * P
FEW = EXPERTS // 2
FT_FEW = -(-FEW * FF // P)
EPS = 1e-5
MASKED = -1000000.0
TILES = PLACES * IMAGES // P
HALF_W = GRID // 2
CHUNKS = TILES // HALF_W
BODY = 2 * HALF_W
AHEAD = 3
PACK = AHEAD + 1
BEHIND = 2
START = BEHIND + 1
TURNS = (TILES - PACK - START) // BODY
HALVES = 2
IPAIRS = IMAGES // 2
PT = 2 * PLACES
HP = PLACES // 2


class Tile:

    def __init__(self, turn, k):
        self.turn, self.k = turn, k

    def plus(self, d):
        return Tile(self.turn, self.k + d)

    def count(self, per, extra):
        return self.turn * (per * BODY) + (per * self.k + extra)

    def looped(self):
        return not isinstance(self.turn, int)

    def real(self):
        return self.looped() or 0 <= self.k < TILES


def until(eng, sem, value):
    if not isinstance(value, int) or value > 0:
        eng.wait_ge(sem, value)


def steps(eng, step):
    for n in range(-PACK, START):
        step(Tile(0, n))
    with eng.Fori(0, TURNS) as turn:
        for n in range(START, START + BODY):
            step(Tile(turn, n))
    for n in range(START + TURNS * BODY, TILES + BEHIND):
        step(Tile(0, n))


class Pair:

    def __init__(self, turn, k):
        self.turn, self.k = turn, k

    def plus(self, d):
        return Pair(self.turn, self.k + d)

    def count(self, per, extra):
        return self.turn * (2 * per) + (per * self.k + extra)

    def number(self):
        return self.k if isinstance(self.turn, int) else None

    def first(self):
        return self.number() == 0

    def last(self):
        return self.number() == IPAIRS - 1


def pairs(eng, pair):
    for k in range(2):
        pair(Pair(0, k))
    with eng.Fori(0, (IPAIRS - 4) // 2) as turn:
        for k in range(2, 4):
            pair(Pair(turn, k))
    for k in range(IPAIRS - 2, IPAIRS):
        pair(Pair(0, k))


def build(nc, x, tok_w, tok_b, wq, wkv, wo, router_w, w1, b1, w2, b2, part_w, out):
    h1_dram = nc.dram_tensor("h1_dram", (IMAGES, PLACES, D), F32, kind="Internal").ap()
    ctx = ExitStack()
    with ctx:
        def sb(name, shape, dt=F32, at=ctx):
            return at.enter_context(nc.sbuf_tensor(name, shape, dt))

        def sem(name):
            return ctx.enter_context(nc.semaphore(name))

        z2T = sb("z2T", [P, IMAGES, PLACES])
        w1_raw = sb("w1_raw", [P, FPAD])
        w2_raw = sb("w2_raw", [P, FT, D])
        ident = sb("ident", [P, P])
        b1_rows = sb("b1_rows", [FT, P])
        b1_col = sb("b1_col", [P, FT])
        b2_sb = sb("b2_sb", [EXPERTS, D])
        router_sb = sb("router_sb", [PARTS, D])
        routerT = sb("routerT", [P, PARTS])
        part_sb = sb("part_sb", [PARTS, EXPERTS])
        eps = sb("eps", [P, 1])

        one = ExitStack()
        xbuf = sb("xbuf", [P, 2, CHANNELS * PATCH, HALF_W * PATCH], at=one)
        patch = sb("patch", [P, 2, CHANNELS * PATCH, PATCH], at=one)
        tw_raw = sb("tw_raw", [P, K_PATCH], at=one)
        wq_raw = sb("wq_raw", [P, PAIRS, D], at=one)
        wk_raw = sb("wk_raw", [P, PAIRS, D], at=one)
        wv_raw = sb("wv_raw", [P, PAIRS, D], at=one)
        wo_raw = sb("wo_raw", [P, HEADS * DH], at=one)
        woT = sb("woT", [P, PAIRS, D], at=one)
        tok_bias = sb("tok_bias", [P, D], at=one)
        twT = sb("twT", [P, KT, D], at=one)
        qk = sb("qk", [P, 2, PAIRS, D], at=one)
        vo = sb("vo", [P, 2, PAIRS, D], at=one)
        mask = sb("mask", [P, HEADS, IMAGES], at=one)
        xT = sb("xT", [P, HALVES, KT // 2, P], at=one)
        h0 = sb("h0", [P, HALF_W, D], at=one)
        z = sb("z", [P, 2, D], at=one)
        zT = sb("zT", [P, HALF_W, P], at=one)
        kq = sb("kq", [P, 2, HEADS, P], at=one)
        vw = sb("vw", [P, 2, 2, PAIRS, D], at=one)
        sm = sb("sm", [P, 2, HEADS, IMAGES], at=one)
        pe_ = sb("pe_", [P, 2, HEADS, IMAGES], at=one)
        pT = sb("pT", [P, PAIRS, P], at=one)
        h1 = sb("h1", [P, 2, D], at=one)
        z2 = sb("z2", [P, 2, D], at=one)
        smax = sb("smax", [P, 2, HEADS], at=one)
        ssum = sb("ssum", [P, 2, HEADS], at=one)
        sinv = sb("sinv", [P, 2, HEADS], at=one)
        stats = sb("stats", [P, 2, 6], at=one)
        moments = sb("moments", [P, 2, 2], at=one)
        lnv = sb("lnv", [P, 2, 1], at=one)
        guess = sb("guess", [P, 2, 1], at=one)
        newt = sb("newt", [P, 2, 2], at=one)
        rstd = sb("rstd", [P, 2, 1], at=one)
        one.close()

        two = ExitStack()
        w1_hi = sb("w1_hi", [P, FPAD], F32R, at=two)
        w1_lo = sb("w1_lo", [P, FPAD], F32R, at=two)
        w2_hi = sb("w2_hi", [P, FT, D], F32R, at=two)
        w2_lo = sb("w2_lo", [P, FT, D], F32R, at=two)
        onehot = sb("onehot", [EXPERTS, FPAD], at=two)
        places = sb("places", [IMAGES, PARTS], at=two)
        zsum = sb("zsum", [P, IMAGES], at=two)
        gate = sb("gate", [IMAGES, 8, 16], at=two)
        gate_idx = sb("gate_idx", [IMAGES, 8], U32, at=two)
        gateT = sb("gateT", [PARTS, IMAGES], at=two)
        ew_raw = sb("ew_raw", [EXPERTS, IMAGES], at=two)
        ew = sb("ew", [EXPERTS, IMAGES], at=two)
        ew_unit = sb("ew_unit", [P, FT, IMAGES], at=two)
        b2w = sb("b2w", [P, IMAGES], at=two)
        late_expert = sb("late_expert", [EXPERTS, 1], at=two)
        late_w = sb("late_w", [1, 2], at=two)
        late_used = sb("late_used", [1, 1], I32, at=two)
        ewp = sb("ewp", [P, 2, FT, 2], at=two)
        b2p = sb("b2p", [P, 2, 2], at=two)
        zp_hi = sb("zp_hi", [P, 2, PT], F32R, at=two)
        zp_lo = sb("zp_lo", [P, 2, PT], F32R, at=two)
        g = sb("g", [P, 4, PT], at=two)
        gw_hi = sb("gw_hi", [P, 4, PT], F32R, at=two)
        gw_lo = sb("gw_lo", [P, 4, PT], F32R, at=two)
        yT = sb("yT", [P, 2, PT], at=two)
        h1_in = sb("h1_in", [HP, 2, 4, D], at=two)
        o_sb = sb("o_sb", [HP, 2, 4, D], at=two)
        two.close()

        bank = [ctx.enter_context(nc.psum_tensor(f"bank{i}", [P, 512], F32)) for i in range(8)]
        xT_ps = bank[0:2]
        wide = bank[2:4]
        s_ps, t_ps, y_ps, h_ps = bank[4:8]

        tw_in, bias_in, attn_w_in, mlp_w_in = sem("tw_in"), sem("bias_in"), sem("attn_w_in"), sem("mlp_w_in")
        x_in = [sem("x_in0"), sem("x_in1")]
        consts, zeroed, prep_pe, prep_ev = sem("consts"), sem("zeroed"), sem("prep_pe"), sem("prep_ev")
        packed = sem("packed")
        xT_ready, xT_done = sem("xT_ready"), sem("xT_done")
        proj_ready, h0_done = sem("proj_ready"), sem("h0_done")
        ln_vec = [sem("ln1_vec"), sem("ln2_vec")]
        ln_act = [sem("ln1_act"), sem("ln2_act")]
        z_ready, zT_ready, zT_done = sem("z_ready"), sem("zT_ready"), sem("zT_done")
        kq_ready, kq_done = sem("kq_ready"), sem("kq_done")
        vw_ready, vw_done = sem("vw_ready"), sem("vw_done")
        s_ready, masked, max_done, shifted, exp_done, sum_done, inv_done, p_ready = \
            sem("s_ready"), sem("masked"), sem("max_done"), sem("shifted"), sem("exp_done"), \
            sem("sum_done"), sem("inv_done"), sem("p_ready")
        pT_ready, pT_done, pv_ready, h1_done = sem("pT_ready"), sem("pT_done"), sem("pv_ready"), sem("h1_done")
        h1_saved = [sem("h1_saved0"), sem("h1_saved1")]
        z2_ready, z2T_ready, z2T_done = sem("z2_ready"), sem("z2T_ready"), sem("z2T_done")
        route_vec, route_pe, route_act, route_pool = \
            sem("route_vec"), sem("route_pe"), sem("route_act"), sem("route_pool")
        w_hi_done, w_lo_done = sem("w_hi_done"), sem("w_lo_done")
        zp_hi_done, zp_ready = sem("zp_hi_done"), sem("zp_ready")
        up_ready, gelu_done, gw_hi_done, gw_ready, down_done = \
            sem("up_ready"), sem("gelu_done"), sem("gw_hi_done"), sem("gw_ready"), sem("down_done")
        late_vec, late_known, ewp_ready = sem("late_vec"), sem("late_known"), sem("ewp_ready")
        yT_done, o_ready, o_done = sem("yT_done"), sem("o_ready"), sem("o_done")
        h1_loaded = [sem("h1_loaded0"), sem("h1_loaded1")]
        o_saved = [sem("o_saved0"), sem("o_saved1")]

        block = ctx.enter_context(nc.Block())

        def load_x(eng, r, half):
            for a in range(2):
                src = x[:, :, bass.ds((2 * r + a) * PATCH, PATCH), half * HALF_W * PATCH:(half + 1) * HALF_W * PATCH]
                src = src.rearrange("b c y w -> b c y w")
                for c in range(CHANNELS):
                    eng.dma_start(xbuf[a * IMAGES:(a + 1) * IMAGES, half, c * PATCH:(c + 1) * PATCH, :],
                                  src[:, c, :, :]).then_inc(x_in[half], 16)
        X_DMAS = 2 * CHANNELS * 16

        def by_use(eng, mlp):
            used = eng.value_load(late_used[0:1, 0:1], min_val=0, max_val=1)
            with eng.If(used < 1):
                mlp(FT_FEW)
            with eng.Else():
                mlp(FT)

        @block.sync
        def _(sp):
            load_x(sp, 0, 0)
            load_x(sp, 0, 1)

            def save_h1(m):
                sp.wait_ge(h1_done, m.count(1, 1))
                r2 = m.k // GRID * 2
                w = m.k % GRID
                for a in range(2):
                    place = m.turn * (2 * GRID) + ((r2 + a) * GRID + w)
                    sp.dma_start(h1_dram[:, bass.ds(place, 1), :].rearrange("b o d -> b (o d)"),
                                 h1[a * IMAGES:(a + 1) * IMAGES, m.k % 2, :]).then_inc(h1_saved[m.k % 2], 16)

            def step(n):
                m = n.plus(AHEAD)
                if m.real() and m.k % HALF_W == HALF_W - 1 and (m.looped() or m.k + BODY < TILES):
                    sp.wait_ge(packed, m.count(1, 1))
                    load_x(sp, m.turn + (m.k // BODY + 1), m.k // HALF_W % 2)
                if n.plus(-1).real():
                    save_h1(n.plus(-1))

            steps(sp, step)
            for k in range(2):
                sp.wait_ge(h1_saved[k], 32 * TILES // 2)

            def load_h1(j):
                if j.number() not in (0, 1):
                    sp.wait_ge(o_done, j.count(1, -1))
                for b in range(2):
                    img = j.count(2, b)
                    sp.dma_start(h1_in[:, j.k % 2, 2 * b:2 * b + 2, :],
                                 h1_dram[bass.ds(img, 1), :, :].rearrange("o (p a) d -> (o p) a d", a=2)
                                 ).then_inc(h1_loaded[j.k % 2], 16)

            def save(j):
                sp.wait_ge(o_done, j.count(1, 1))
                for b in range(2):
                    img = j.count(2, b)
                    sp.dma_start(out[bass.ds(img, 1), :, :].rearrange("o (p a) d -> (o p) a d", a=2),
                                 o_sb[:, j.k % 2, 2 * b:2 * b + 2, :]).then_inc(o_saved[j.k % 2], 16)

            def pair(j):
                load_h1(j)
                if not j.first():
                    save(j.plus(-1))
                if j.last():
                    save(j)
            pairs(sp, pair)
            for k in range(2):
                sp.wait_ge(o_saved[k], 32 * IPAIRS // 2)

        @block.gpsimd
        def _(pool):
            pool.memset(ident[:, :], 0.0).then_inc(zeroed, 1)
            pool.memset(mask[:, :, :], 3.0e38).then_inc(zeroed, 1)
            pool.memset(eps[:, :], EPS).then_inc(consts, 1)
            pool.memset(b1_rows[:, :], 0.0).then_inc(zeroed, 1)
            pool.memset(w1_raw[:, EXPERTS * FF:FPAD], 0.0).then_inc(zeroed, 1)
            pool.memset(w2_raw[:, FT - 1, :], 0.0).then_inc(zeroed, 1)
            pool.wait_ge(zeroed, 5)
            pool.affine_select(out=ident[:, :], in_=ident[:, :], compare_op=ALU.not_equal, fill=1.0,
                               base=0, pattern=[[-1, P]], channel_multiplier=1).then_inc(consts, 1)
            for a in range(2):
                pool.wait_ge(consts, 2 + a)
                m = mask[a * IMAGES:(a + 1) * IMAGES, :, :]
                pool.affine_select(out=m, in_=m, compare_op=ALU.is_ge, fill=MASKED, base=0,
                                   pattern=[[0, HEADS], [-1, IMAGES]], channel_multiplier=1).then_inc(consts, 1)

            pool.wait_ge(consts, 4)

            def step(n):
                b = n.k % 2
                if n.real():
                    pool.wait_ge(max_done, n.count(1, 1))
                    pool.tensor_tensor(sm[:, b, :, :], sm[:, b, :, :],
                                       smax[:, b, :].unsqueeze(2).to_broadcast([P, HEADS, IMAGES]),
                                       ALU.subtract).then_inc(shifted, 1)
                if n.real():
                    pool.wait_ge(inv_done, n.count(1, 1))
                    pool.tensor_tensor(pe_[:, b, :, :], pe_[:, b, :, :],
                                       sinv[:, b, :].unsqueeze(2).to_broadcast([P, HEADS, IMAGES]),
                                       ALU.mult).then_inc(p_ready, 1)
            steps(pool, step)

            pool.wait_ge(z2T_done, TILES)
            for k in range(2):
                pool.wait_ge(h1_saved[k], 32 * TILES // 2)
            pool.memset(onehot[:, :], 1.0).then_inc(route_pool, 1)
            pool.iota(places[:, :], pattern=[[1, PARTS]], base=0, channel_multiplier=0,
                      allow_small_or_imprecise_dtypes=True).then_inc(route_pool, 1)
            pool.wait_ge(route_pool, 2)
            pool.affine_select(out=onehot[:, :], in_=onehot[:, :], compare_op=ALU.is_ge, fill=0.0, base=0,
                               pattern=[[1, FPAD]], channel_multiplier=-FF).then_inc(route_pool, 1)
            pool.wait_ge(route_pool, 3)
            pool.affine_select(out=onehot[:, :], in_=onehot[:, :], compare_op=ALU.is_ge, fill=0.0, base=FF - 1,
                               pattern=[[-1, FPAD]], channel_multiplier=FF).then_inc(route_pool, 1)
            pool.memset(late_expert[:, :], 1.0).then_inc(route_pool, 1)
            pool.wait_ge(route_pool, 5)
            pool.affine_select(out=late_expert[:, :], in_=late_expert[:, :], compare_op=ALU.is_ge, fill=0.0,
                               base=-FEW, pattern=[[0, 1]], channel_multiplier=1).then_inc(route_pool, 1)

            def mlp(tiles):
                def weigh(j, t):
                    pool.wait_ge(gelu_done, j.count(tiles, t + 1))
                    if not (j.first() and t < 4):
                        pool.wait_ge(down_done, j.count(tiles, t - 3))
                    if t == 0:
                        pool.wait_ge(ewp_ready, j.count(1, 1))
                    pool.tensor_tensor(gw_hi[:, t % 4, :].rearrange("p (b s) -> p b s", b=2),
                                       g[:, t % 4, :].rearrange("p (b s) -> p b s", b=2),
                                       ewp[:, j.k % 2, t, :].unsqueeze(2).to_broadcast([P, 2, PLACES]),
                                       ALU.mult).then_inc(gw_hi_done, 1)

                def pair(j):
                    for t in range(tiles):
                        weigh(j, t)
                pairs(pool, pair)

            pool.wait_ge(late_known, 1)
            by_use(pool, mlp)

        @block.scalar
        def _(act):
            act.dma_start(tw_raw[:, :], tok_w).then_inc(tw_in, 16)
            act.dma_start(tok_bias[:, :], tok_b.partition_broadcast(P)).then_inc(bias_in, 16)
            for dst, src in ((wq_raw, wq), (wk_raw, wkv[0:HEADS * DH, :]), (wv_raw, wkv[HEADS * DH:2 * HEADS * DH, :])):
                act.dma_start(dst[:, :, :], src.rearrange("(t p) j -> p t j", p=P)).then_inc(attn_w_in, 16)
            act.dma_start(wo_raw[:, :], wo).then_inc(attn_w_in, 16)
            act.wait_ge(zeroed, 5)
            full = (FT - 1) * P
            rest = EXPERTS * FF - full
            act.dma_start(w1_raw[:, 0:EXPERTS * FF].rearrange("p (e f) -> p e f", e=EXPERTS),
                          w1.rearrange("e d f -> d e f")).then_inc(mlp_w_in, 16)
            w2_rows = w2.rearrange("e f d -> (e f) d")
            act.dma_start(w2_raw[:, 0:FT - 1, :], w2_rows[0:full, :].rearrange("(t p) d -> p t d", p=P)).then_inc(mlp_w_in, 16)
            act.dma_start(w2_raw[0:rest, FT - 1, :], w2_rows[full:full + rest, :]).then_inc(mlp_w_in, 16)
            b1_flat = b1.rearrange("e f -> (e f)")
            act.dma_start(b1_rows[0:FT - 1, :], b1_flat[0:full].rearrange("(t p) -> t p", p=P)).then_inc(mlp_w_in, 16)
            act.dma_start(b1_rows[FT - 1:FT, 0:rest], b1_flat[full:full + rest].rearrange("(o p) -> o p", o=1)).then_inc(mlp_w_in, 16)
            act.dma_start(b2_sb[:, :], b2).then_inc(mlp_w_in, 16)
            act.dma_start(router_sb[:, :], router_w).then_inc(mlp_w_in, 16)
            act.dma_start(part_sb[:, :], part_w).then_inc(mlp_w_in, 16)

            nc.scalar.preload_act_table_set("natural_log_exp_and_others")
            for i in range(2):
                act.wait_ge(prep_pe, i + 1)
                act.activation(twT[:, 3 * i:3 * i + 3, :], bank[i][:, 0:3 * P].rearrange("p (k e) -> p k e", e=D),
                               ACT.Copy).then_inc(prep_ev, 1)
            for q in range(2):
                act.wait_ge(prep_pe, 4 + q)
                act.activation(qk[:, q, :, :], bank[4 + q][:, :].rearrange("p (k e) -> p k e", e=D),
                               ACT.Copy, scale=DH ** -0.5).then_inc(prep_ev, 1)

            def log(m, which):
                act.wait_ge(ln_vec[which], m.count(5, 2))
                act.activation(lnv[:, which, :], moments[:, which, 1:2], ACT.Ln, bias=eps[:, 0:1]).then_inc(ln_act[which], 1)

            def exp(m, which):
                act.wait_ge(ln_act[which], m.count(2, 1))
                act.activation(guess[:, which, :], lnv[:, which, :], ACT.Exp, scale=-0.5).then_inc(ln_act[which], 1)

            def take_x(m, h):
                act.wait_ge(xT_ready, m.count(2, h + 1))
                until(act, proj_ready, m.count(1, 0))
                act.activation(xT[:, h, :, :], xT_ps[h][:, 0:3 * P].rearrange("p (k t) -> p k t", t=P),
                               ACT.Copy).then_inc(xT_done, 1)

            def take_vw(n, a):
                act.wait_ge(vw_ready, n.count(2, a + 1))
                if a == 0:
                    until(act, pv_ready, n.count(1, -1))
                act.activation(vw[:, n.k % 2, a, :, :], wide[a][:, :].rearrange("p (t f) -> p t f", f=D),
                               ACT.Copy).then_inc(vw_done, 1)

            def take_kq(m, a):
                act.wait_ge(kq_ready, m.count(2, a + 1))
                act.activation(kq[:, m.k % 2, 4 * a:4 * a + 4, :], wide[a][:, :].rearrange("p (h t) -> p h t", t=P),
                               ACT.Copy).then_inc(kq_done, 1)

            act.wait_ge(consts, 1)

            def step(n):
                emb, nrm, key, prev, last = n.plus(AHEAD), n.plus(2), n.plus(1), n.plus(-1), n.plus(-BEHIND)
                if emb.real():
                    take_x(emb, 0)
                if nrm.real():
                    act.wait_ge(zT_ready, nrm.count(1, 1))
                    act.activation(zT[:, nrm.k % HALF_W, :], t_ps[:, 0:P], ACT.Copy).then_inc(zT_done, 1)
                if last.real():
                    log(last, 1)
                if emb.real():
                    take_x(emb, 1)
                if last.real():
                    exp(last, 1)
                if n.real():
                    take_vw(n, 0)
                    act.wait_ge(shifted, n.count(1, 1))
                    until(act, pT_ready, n.count(1, -1))
                    act.activation(pe_[:, n.k % 2, :, :], sm[:, n.k % 2, :, :], ACT.Exp).then_inc(exp_done, 1)
                    take_vw(n, 1)
                if prev.real():
                    act.wait_ge(pT_ready, prev.count(1, 1))
                    act.activation(pT[:, :, :], t_ps[:, :].rearrange("p (t q) -> p t q", q=P), ACT.Copy).then_inc(pT_done, 1)
                if key.real():
                    until(act, s_ready, key.count(1, -1))
                    take_kq(key, 0)
                    take_kq(key, 1)
                if emb.real():
                    log(emb, 0)
                    exp(emb, 0)
                if last.real():
                    act.wait_ge(z2T_ready, last.count(1, 1))
                    w0 = last.turn * (2 * GRID) + (last.k // GRID * 2 * GRID + last.k % GRID)
                    for a in range(2):
                        act.activation(z2T[:, :, bass.ds(w0 + a * GRID, 1)].rearrange("p b o -> p (b o)"),
                                       h_ps[:, a * IMAGES:(a + 1) * IMAGES], ACT.Copy).then_inc(z2T_done, 1)
            steps(act, step)

            act.wait_ge(mlp_w_in, 8 * 16)
            act.wait_ge(p_ready, TILES)
            act.wait_ge(h1_saved[0], 32 * TILES // 2)
            act.wait_ge(h1_saved[1], 32 * TILES // 2)
            act.activation(w1_hi[:, :], w1_raw[:, :], ACT.Copy).then_inc(w_hi_done, 1)
            act.activation(w2_hi[:, :, :], w2_raw[:, :, :], ACT.Copy).then_inc(w_hi_done, 1)
            act.wait_ge(route_vec, 3)
            act.activation(gate[:, 1, 0:PARTS], gate[:, 0, 0:PARTS], ACT.Exp, bias=gate[:, 2, 8:9]).then_inc(route_act, 1)

            def mlp(tiles):
                def gelu(j, t):
                    act.wait_ge(up_ready, j.count(tiles, t + 1))
                    if not (j.first() and t < 4):
                        act.wait_ge(gw_ready, j.count(tiles, t - 3))
                    act.activation(g[:, t % 4, :], bank[t % 4][:, 0:PT], ACT.Gelu,
                                   bias=b1_col[:, t:t + 1]).then_inc(gelu_done, 1)

                def split_z(j):
                    until(act, up_ready, j.count(tiles, -tiles))
                    act.activation(zp_hi[:, j.k % 2, :],
                                   z2T[:, bass.ds(j.count(2, 0), 2), :].rearrange("p b t -> p (b t)"),
                                   ACT.Copy).then_inc(zp_hi_done, 1)

                def take_y(j):
                    act.wait_ge(down_done, j.count(tiles, tiles))
                    if not j.first():
                        act.wait_ge(o_ready, j.count(1, 0))
                    for b in range(2):
                        act.activation(yT[:, j.k % 2, b * PLACES:(b + 1) * PLACES],
                                       bank[4 + j.k % 2][:, b * PLACES:(b + 1) * PLACES], ACT.Identity,
                                       bias=b2p[:, j.k % 2, b:b + 1]).then_inc(yT_done, 1)

                def pair(j):
                    for t in range(tiles):
                        gelu(j, t)
                        if t == 1 and not j.last():
                            split_z(j.plus(1))
                        if t == 3 and not j.first():
                            take_y(j.plus(-1))
                    if j.last():
                        take_y(j)
                pairs(act, pair)

            act.activation(zp_hi[:, 0, :], z2T[:, 0:2, :].rearrange("p b t -> p (b t)"), ACT.Copy).then_inc(zp_hi_done, 1)
            act.wait_ge(route_vec, 19)
            act.wait_ge(late_known, 1)
            by_use(act, mlp)

        @block.tensor
        def _(pe):
            def mm3(o, a_hi, a_lo, b_hi, b_lo, start, stop):
                pe.matmul(o, a_hi, b_hi, start=start, stop=False)
                pe.matmul(o, a_lo, b_hi, start=False, stop=False)
                return pe.matmul(o, a_hi, b_lo, start=False, stop=stop)

            pe.wait_ge(consts, 4)
            pe.wait_ge(tw_in, 16)
            for i in range(2):
                for k in range(3):
                    mm = pe.transpose(bank[i][:, k * P:(k + 1) * P], tw_raw[:, (3 * i + k) * P:(3 * i + k + 1) * P], ident[:, :])
                mm.then_inc(prep_pe, 1)
            pe.wait_ge(attn_w_in, 4 * 16)
            for t in range(PAIRS):
                mm = pe.transpose(bank[2][:, t * P:(t + 1) * P], wo_raw[:, t * P:(t + 1) * P], ident[:, :])
            mm.then_inc(prep_pe, 1)
            for q in range(2):
                for t in range(PAIRS):
                    r = slice(q * DH, (q + 1) * DH)
                    mm = pe.matmul(bank[4 + q][:, t * P:(t + 1) * P], wk_raw[r, t, :], wq_raw[r, t, :], start=True, stop=True)
                mm.then_inc(prep_pe, 1)
            pe.wait_ge(prep_ev, 5)
            for q in range(2):
                for t in range(PAIRS):
                    r = slice(q * DH, (q + 1) * DH)
                    mm = pe.matmul(bank[6 + q][:, t * P:(t + 1) * P], wv_raw[r, t, :], woT[r, t, :], start=True, stop=True)
                mm.then_inc(prep_pe, 1)
            pe.wait_ge(mlp_w_in, 8 * 16)
            pe.transpose(bank[3][:, 0:FT], b1_rows[:, :], ident[0:FT, 0:FT])
            pe.transpose(bank[3][:, 64:64 + PARTS], router_sb[:, :], ident[0:PARTS, 0:PARTS]).then_inc(prep_pe, 1)
            pe.wait_ge(prep_ev, 9)

            def turn_x(m, h):
                if h == 0:
                    pe.wait_ge(packed, m.count(1, 1))
                until(pe, xT_done, m.count(2, h - 1))
                for k in range(3):
                    row = (3 * h + k) * ROWS8
                    mm = pe.transpose(xT_ps[h][:, k * P:(k + 1) * P],
                                      patch[:, m.k % 2, row:row + ROWS8, :].rearrange("p r c -> p (r c)"), ident[:, :])
                mm.then_inc(xT_ready, 1)

            def project(m):
                pe.wait_ge(xT_done, m.count(2, 2))
                until(pe, z2T_done, m.count(2, -2 * 5))
                for k in range(KT):
                    h, kk = k // 3, k % 3
                    mm = pe.matmul(h_ps[:, 0:D], xT[:, h, kk, :], twT[:, k, :], start=(k == 0), stop=(k == KT - 1))
                mm.then_inc(proj_ready, 1)

            def turn_z(m):
                pe.wait_ge(z_ready, m.count(1, 1))
                until(pe, pT_done, m.count(1, -3))
                pe.transpose(t_ps[:, 0:P], z[:, m.k % 2, :], ident[:, :]).then_inc(zT_ready, 1)

            def keys(m, a):
                if a == 0:
                    pe.wait_ge(zT_done, m.count(1, 1))
                if n_real_before(m):
                    until(pe, vw_done, m.count(2, -1 + a))
                for h in range(4):
                    t, q = (4 * a + h) // 2, h % 2
                    mm = pe.matmul(wide[a][:, h * P:(h + 1) * P], qk[:, q, t, :], zT[:, m.k % HALF_W, :],
                                   start=True, stop=True)
                mm.then_inc(kq_ready, 1)

            def n_real_before(m):
                return m.looped() or m.k >= 1

            def values(n, a):
                pe.wait_ge(kq_done, n.count(2, a + 1))
                lhs = zT[:, n.k % HALF_W, a * IMAGES:(a + 1) * IMAGES]
                for q in range(2):
                    mm = pe.matmul(wide[a][q * IMAGES:(q + 1) * IMAGES, :], lhs, vo[:, q, :, :], start=True, stop=True)
                mm.then_inc(vw_ready, 1)

            def scores(n):
                pe.wait_ge(kq_done, n.count(2, 2))
                until(pe, masked, n.count(1, 0))
                for a in range(2):
                    t = slice(a * IMAGES, (a + 1) * IMAGES)
                    mm = pe.matmul(s_ps[t, :], zT[:, n.k % HALF_W, t], kq[:, n.k % 2, :, t], start=True, stop=True)
                mm.then_inc(s_ready, 1)

            def turn_p(m):
                pe.wait_ge(p_ready, m.count(1, 1))
                pe.wait_ge(zT_done, m.count(1, 4) if m.looped() else min(m.k + 4, TILES))
                for t in range(PAIRS):
                    mm = pe.transpose(t_ps[:, t * P:(t + 1) * P], pe_[:, m.k % 2, 2 * t:2 * t + 2, :].rearrange("p h k -> p (h k)"), ident[:, :])
                mm.then_inc(pT_ready, 1)

            def mix(m):
                pe.wait_ge(pT_done, m.count(1, 1))
                pe.wait_ge(vw_done, m.count(2, 2))
                until(pe, h1_done, m.count(1, 0))
                for t in range(PAIRS):
                    for a in range(2):
                        s = slice(a * IMAGES, (a + 1) * IMAGES)
                        mm = pe.matmul(y_ps[s, 0:D], pT[:, t, s], vw[:, m.k % 2, a, t, :],
                                       start=(t == 0), stop=(t == PAIRS - 1))
                mm.then_inc(pv_ready, 1)

            def turn_z2(m):
                pe.wait_ge(z2_ready, m.count(1, 1))
                h0_seen = m.count(1, 6) if m.looped() else min(m.k + 6, TILES)
                pe.wait_ge(h0_done, h0_seen)
                pe.transpose(h_ps[:, 0:P], z2[:, m.k % 2, :], ident[:, :]).then_inc(z2T_ready, 1)

            def step(n):
                emb, nrm, key, prev, last = n.plus(AHEAD), n.plus(2), n.plus(1), n.plus(-1), n.plus(-BEHIND)
                if n.real():
                    scores(n)
                if emb.real():
                    turn_x(emb, 0)
                if nrm.real():
                    turn_z(nrm)
                if n.real():
                    values(n, 0)
                if emb.real():
                    turn_x(emb, 1)
                if n.real():
                    values(n, 1)
                if prev.real():
                    turn_p(prev)
                if key.real():
                    keys(key, 0)
                if emb.real():
                    project(emb)
                if key.real():
                    keys(key, 1)
                if prev.real():
                    mix(prev)
                if last.real():
                    turn_z2(last)
            steps(pe, step)

            pe.wait_ge(route_vec, 1)
            pe.wait_ge(z2T_done, 2 * TILES)
            pe.matmul(bank[6][0:IMAGES, 0:PARTS], zsum[:, :], routerT[:, :], start=True, stop=True).then_inc(route_pe, 1)
            pe.wait_ge(route_vec, 13)
            pe.transpose(bank[6][0:PARTS, 0:IMAGES], gate[:, 7, 0:PARTS], ident[0:IMAGES, 0:IMAGES]).then_inc(route_pe, 1)
            pe.wait_ge(route_vec, 14)
            pe.matmul(bank[6][0:EXPERTS, 0:IMAGES], part_sb[:, :], gateT[:, :], start=True, stop=True).then_inc(route_pe, 1)
            pe.wait_ge(route_vec, 16)
            pe.wait_ge(route_pool, 4)
            pe.wait_ge(route_pool, 6)
            pe.matmul(bank[7][0:1, 0:IMAGES], late_expert[:, :], ew[:, :], start=True, stop=True).then_inc(route_pe, 1)
            for t in range(FT):
                mm = pe.matmul(bank[4 + t // 8][:, t % 8 * IMAGES:(t % 8 + 1) * IMAGES], onehot[:, t * P:(t + 1) * P],
                               ew[:, :], start=True, stop=True)
            pe.matmul(bank[6][:, 0:IMAGES], b2_sb[:, :], ew[:, :], start=True, stop=True).then_inc(route_pe, 1)
            pe.wait_ge(w_lo_done, 2)

            def mlp(tiles):
                def up(j, t):
                    if t == 0:
                        pe.wait_ge(zp_ready, j.count(1, 1))
                    if not (j.first() and t < 4):
                        pe.wait_ge(gelu_done, j.count(tiles, t - 3))
                    f = slice(t * P, (t + 1) * P)
                    mm3(bank[t % 4][:, 0:PT], w1_hi[:, f], w1_lo[:, f], zp_hi[:, j.k % 2, :], zp_lo[:, j.k % 2, :],
                        True, True).then_inc(up_ready, 1)

                def down(j, t):
                    pe.wait_ge(gw_ready, j.count(tiles, t + 1))
                    if t == 0 and j.number() not in (0, 1):
                        pe.wait_ge(yT_done, j.count(2, -2))
                    mm = mm3(bank[4 + j.k % 2][:, 0:PT], w2_hi[:, t, :], w2_lo[:, t, :], gw_hi[:, t % 4, :],
                             gw_lo[:, t % 4, :], t == 0, t == tiles - 1)
                    mm.then_inc(down_done, 1)
                    return mm

                def turn_y(j):
                    pe.wait_ge(yT_done, j.count(2, 2))
                    if not j.first():
                        pe.wait_ge(o_done, j.count(1, 0))
                    for b in range(2):
                        for a in range(2):
                            c = 2 * b + a
                            mm = pe.transpose(bank[6][0:HP, c * D:(c + 1) * D],
                                              yT[:, j.k % 2, b * PLACES + a:(b + 1) * PLACES:2], ident[:, :])
                    mm.then_inc(o_ready, 1)

                lead = 3
                for t in range(lead):
                    up(Pair(0, 0), t)

                def pair(j):
                    for t in range(tiles):
                        if t + lead < tiles:
                            up(j, t + lead)
                        elif not j.last():
                            up(j.plus(1), t + lead - tiles)
                        down(j, t)
                        if t == 5 and not j.first():
                            turn_y(j.plus(-1))
                    if j.last():
                        turn_y(j)
                pairs(pe, pair)

            pe.wait_ge(route_vec, 19)
            pe.wait_ge(late_known, 1)
            by_use(pe, mlp)

        @block.vector
        def _(dve):
            dve.wait_ge(prep_pe, 3)
            dve.tensor_copy(woT[:, :, :], bank[2][:, :].rearrange("p (t f) -> p t f", f=D)).then_inc(prep_ev, 1)
            for q in range(2):
                dve.wait_ge(prep_pe, 6 + q)
                dve.tensor_copy(vo[:, q, :, :], bank[6 + q][:, :].rearrange("p (t f) -> p t f", f=D)).then_inc(prep_ev, 1)
            dve.wait_ge(prep_pe, 8)
            dve.tensor_copy(b1_col[:, :], bank[3][:, 0:FT]).then_inc(prep_ev, 1)
            dve.tensor_copy(routerT[:, :], bank[3][:, 64:64 + PARTS]).then_inc(prep_ev, 1)
            dve.wait_ge(bias_in, 16)
            dve.wait_ge(consts, 4)

            def stats_of(which, src):
                dve.bn_stats(stats[:, which, :], src).then_inc(ln_vec[which], 1)

            def moments_of(which):
                dve.bn_aggr(moments[:, which, :], stats[:, which, :]).then_inc(ln_vec[which], 1)

            def norm_apply(m, which, src, dst, done):
                y = guess[:, which, 0:1]
                dve.wait_ge(ln_act[which], m.count(2, 2))
                dve.tensor_scalar(newt[:, which, 0:1], moments[:, which, 1:2], EPS, y, ALU.add, ALU.mult).then_inc(ln_vec[which], 1)
                dve.wait_ge(ln_vec[which], m.count(5, 3))
                dve.tensor_scalar(newt[:, which, 1:2], newt[:, which, 0:1], y, -0.5, ALU.mult, ALU.mult).then_inc(ln_vec[which], 1)
                dve.wait_ge(ln_vec[which], m.count(5, 4))
                dve.tensor_scalar(rstd[:, which, :], newt[:, which, 1:2], 1.5, y, ALU.add, ALU.mult).then_inc(ln_vec[which], 1)
                dve.wait_ge(ln_vec[which], m.count(5, 5))
                dve.tensor_scalar(dst, src, moments[:, which, 0:1], rstd[:, which, 0:1], ALU.subtract, ALU.mult).then_inc(done, 1)

            def pack(m):
                c, w = m.k // HALF_W % 2, m.k % HALF_W
                if w == 0:
                    dve.wait_ge(x_in[c], m.turn * X_DMAS + X_DMAS * (m.k // BODY + 1))
                until(dve, xT_ready, m.count(2, -2))
                dve.tensor_copy(patch[:, m.k % 2, :, :], xbuf[:, c, :, w * PATCH:(w + 1) * PATCH]).then_inc(packed, 1)

            def step(n):
                emb, last = n.plus(AHEAD), n.plus(-BEHIND)
                b = n.k % 2
                if last.real():
                    dve.wait_ge(pv_ready, last.count(1, 1))
                    k = last.k // 2
                    until(dve, h1_saved[last.k % 2], last.turn * (16 * BODY) + 32 * k)
                    dve.tensor_tensor(h1[:, last.k % 2, :], y_ps[:, 0:D], h0[:, last.k % HALF_W, :], ALU.add).then_inc(h1_done, 1)
                    dve.wait_ge(h1_done, last.count(1, 1))
                    stats_of(1, h1[:, last.k % 2, :])
                    until(dve, ln_vec[1], last.count(5, 1))
                if n.real():
                    dve.wait_ge(s_ready, n.count(1, 1))
                    until(dve, exp_done, n.count(1, -1))
                    dve.tensor_tensor(sm[:, b, :, :], s_ps[:, :].rearrange("p (h k) -> p h k", k=IMAGES),
                                      mask[:, :, :], ALU.min).then_inc(masked, 1)
                if last.real():
                    moments_of(1)
                if n.real():
                    dve.wait_ge(masked, n.count(1, 1))
                    dve.tensor_reduce(smax[:, b, :], sm[:, b, :, :], AX.X, ALU.max).then_inc(max_done, 1)
                if last.real():
                    norm_apply(last, 1, h1[:, last.k % 2, :], z2[:, last.k % 2, :], z2_ready)
                if n.real():
                    dve.wait_ge(exp_done, n.count(1, 1))
                    dve.tensor_reduce(ssum[:, b, :], pe_[:, b, :, :], AX.X, ALU.add).then_inc(sum_done, 1)
                if n.real():
                    dve.wait_ge(sum_done, n.count(1, 1))
                    dve.reciprocal(sinv[:, b, :], ssum[:, b, :]).then_inc(inv_done, 1)
                if emb.real():
                    dve.wait_ge(proj_ready, emb.count(1, 1))
                    dve.tensor_tensor(h0[:, emb.k % HALF_W, :], h_ps[:, 0:D], tok_bias[:, :], ALU.add).then_inc(h0_done, 1)
                    dve.wait_ge(h0_done, emb.count(1, 1))
                    stats_of(0, h0[:, emb.k % HALF_W, :])
                    dve.wait_ge(ln_vec[0], emb.count(5, 1))
                if n.plus(PACK).real():
                    pack(n.plus(PACK))
                if emb.real():
                    moments_of(0)
                    norm_apply(emb, 0, h0[:, emb.k % HALF_W, :], z[:, emb.k % 2, :], z_ready)
            steps(dve, step)

            rv = [0]

            def link(ins):
                rv[0] += 1
                ins.then_inc(route_vec, 1)

            dve.wait_ge(z2T_done, 2 * TILES)
            dve.wait_ge(p_ready, TILES)
            dve.wait_ge(h1_saved[0], 32 * TILES // 2)
            dve.wait_ge(h1_saved[1], 32 * TILES // 2)
            link(dve.tensor_reduce(zsum[:, :], z2T[:, :, :], AX.X, ALU.add))
            dve.wait_ge(w_hi_done, 1)
            dve.tensor_tensor(w1_lo[:, :], w1_raw[:, :], w1_hi[:, :].bitcast(F32), ALU.subtract).then_inc(w_lo_done, 1)
            dve.wait_ge(w_hi_done, 2)
            dve.tensor_tensor(w2_lo[:, :, :], w2_raw[:, :, :], w2_hi[:, :, :].bitcast(F32), ALU.subtract).then_inc(w_lo_done, 1)
            dve.wait_ge(route_pe, 1)
            link(dve.tensor_scalar(gate[:, 0, 0:PARTS], bank[6][0:IMAGES, 0:PARTS], 1.0 / PLACES, None, ALU.mult))
            dve.wait_ge(route_vec, 2)
            link(dve.tensor_reduce(gate[:, 2, 8:9], gate[:, 0, 0:PARTS], AX.X, ALU.max, negate=True))
            dve.wait_ge(route_act, 1)
            link(dve.tensor_reduce(gate[:, 2, 9:10], gate[:, 1, 0:PARTS], AX.X, ALU.add))
            dve.wait_ge(route_vec, 4)
            link(dve.reciprocal(gate[:, 2, 10:11], gate[:, 2, 9:10]))
            dve.wait_ge(route_vec, 5)
            link(dve.tensor_scalar(gate[:, 3, 0:PARTS], gate[:, 1, 0:PARTS], gate[:, 2, 10:11], None, ALU.mult))
            dve.wait_ge(route_vec, 6)
            link(dve.max(gate[:, 4, 0:8], gate[:, 3, 0:PARTS]))
            dve.wait_ge(route_vec, 7)
            link(dve.max_index(gate_idx[:, :], gate[:, 4, 0:8], gate[:, 3, 0:PARTS]))
            link(dve.tensor_tensor(gate[:, 2, 11:12], gate[:, 4, 0:1], gate[:, 4, 1:2], ALU.add))
            dve.wait_ge(route_vec, 9)
            link(dve.reciprocal(gate[:, 2, 12:13], gate[:, 2, 11:12]))
            link(dve.tensor_copy(gate[:, 2, 14:16], gate_idx[:, 0:2]))
            dve.wait_ge(route_vec, 11)
            dve.wait_ge(route_pool, 2)
            link(dve.tensor_scalar(gate[:, 5, 0:PARTS], places[:, :], gate[:, 2, 14:15], gate[:, 4, 0:1], ALU.is_equal, ALU.mult))
            dve.tensor_scalar(gate[:, 6, 0:PARTS], places[:, :], gate[:, 2, 15:16], gate[:, 4, 1:2],
                              ALU.is_equal, ALU.mult).then_inc(w_lo_done, 1)
            dve.wait_ge(route_vec, 12)
            dve.wait_ge(w_lo_done, 3)
            dve.tensor_tensor(gate[:, 7, 0:PARTS], gate[:, 5, 0:PARTS], gate[:, 6, 0:PARTS], ALU.add).then_inc(w_lo_done, 1)
            dve.wait_ge(w_lo_done, 4)
            link(dve.tensor_scalar(gate[:, 7, 0:PARTS], gate[:, 7, 0:PARTS], gate[:, 2, 12:13], None, ALU.mult))
            dve.wait_ge(route_pe, 2)
            link(dve.tensor_copy(gateT[:, :], bank[6][0:PARTS, 0:IMAGES]))
            dve.wait_ge(route_pe, 3)
            link(dve.tensor_copy(ew_raw[:, :], bank[6][0:EXPERTS, 0:IMAGES]))
            dve.wait_ge(route_vec, 15)
            link(dve.scalar_tensor_tensor(out=ew[:, :], in0=ew_raw[:, :], scalar=1e-6, in1=ew_raw[:, :],
                                          op0=ALU.is_gt, op1=ALU.mult))
            dve.wait_ge(route_pe, 4)
            dve.tensor_reduce(late_w[:, 0:1], bank[7][0:1, 0:IMAGES], AX.X, ALU.add).then_inc(late_vec, 1)
            dve.wait_ge(late_vec, 1)
            dve.tensor_scalar(late_used[:, :], late_w[:, 0:1], 0.0, None, ALU.is_gt).then_inc(late_known, 1)
            dve.wait_ge(route_pe, 5)
            for i in range(2):
                link(dve.tensor_copy(ew_unit[:, 8 * i:8 * i + 8, :],
                                     bank[4 + i][:, :].rearrange("p (t b) -> p t b", b=IMAGES)))
            link(dve.tensor_copy(b2w[:, :], bank[6][:, 0:IMAGES]))
            dve.wait_ge(route_vec, 19)

            def weights_of(j):
                img = j.count(2, 0)
                dve.tensor_copy(b2p[:, j.k % 2, :], b2w[:, bass.ds(img, 2)])
                dve.tensor_copy(ewp[:, j.k % 2, :, :], ew_unit[:, :, bass.ds(img, 2)]).then_inc(ewp_ready, 1)

            def split_z(j):
                b = j.k % 2
                src = z2T[:, bass.ds(j.count(2, 0), 2), :].rearrange("p b t -> p (b t)")
                dve.wait_ge(zp_hi_done, j.count(1, 1))
                dve.tensor_tensor(zp_lo[:, b, :], src, zp_hi[:, b, :].bitcast(F32), ALU.subtract).then_inc(zp_ready, 1)

            def add_h1(j):
                dve.wait_ge(o_ready, j.count(1, 1))
                k = j.k // 2
                dve.wait_ge(h1_loaded[j.k % 2], j.turn * 32 + 32 * (k + 1))
                until(dve, o_saved[j.k % 2], j.turn * 32 + 32 * k)
                dve.tensor_tensor(o_sb[:, j.k % 2, :, :], bank[6][0:HP, :].rearrange("p (c d) -> p c d", d=D),
                                  h1_in[:, j.k % 2, :, :], ALU.add).then_inc(o_done, 1)

            def mlp(tiles):
                def weigh(j, t):
                    dve.wait_ge(gw_hi_done, j.count(tiles, t + 1))
                    if not (j.first() and t < 4):
                        dve.wait_ge(down_done, j.count(tiles, t - 3))
                    if t == 0:
                        dve.wait_ge(ewp_ready, j.count(1, 1))
                    for b in range(2):
                        s = slice(b * PLACES, (b + 1) * PLACES)
                        lo = dve.scalar_tensor_tensor(out=gw_lo[:, t % 4, s], in0=g[:, t % 4, s],
                                                      scalar=ewp[:, j.k % 2, t, b:b + 1],
                                                      in1=gw_hi[:, t % 4, s].bitcast(F32), op0=ALU.mult,
                                                      op1=ALU.subtract)
                    lo.then_inc(gw_ready, 1)

                def pair(j):
                    for t in range(tiles):
                        weigh(j, t)
                        if t == 2 and not j.last():
                            split_z(j.plus(1))
                        if t == 4 and not j.last():
                            weights_of(j.plus(1))
                        if t == 6 and not j.first():
                            add_h1(j.plus(-1))
                    if j.last():
                        add_h1(j)
                pairs(dve, pair)

            split_z(Pair(0, 0))
            weights_of(Pair(0, 0))
            by_use(dve, mlp)


_INS = ['x', 'L0_tok_w', 'L0_tok_b', 'L0_attn_Wq', 'L0_attn_Wkv', 'L0_attn_Wo', 'L0_ffn_router_w', 'L0_ffn_W1',
        'L0_ffn_b1', 'L0_ffn_W2', 'L0_ffn_b2']
_PARTITIONS = [(6,), (5, 1), (4, 2), (4, 1, 1), (3, 3), (3, 2, 1), (3, 1, 1, 1), (2, 2, 2), (2, 2, 1, 1),
               (2, 1, 1, 1, 1), (1, 1, 1, 1, 1, 1)]


def kernel(**inputs):
    import numpy as _np
    import concourse.bacc as _bacc
    from concourse import mybir as _mybir
    from concourse.bass_utils import run_bass_kernel_spmd as _run

    nc = _bacc.Bacc("TRN2", target_bir_lowering=False, num_devices=1)
    arrays, args = {}, []
    for name in _INS:
        a = _np.ascontiguousarray(inputs[name])
        arrays[f"in_{name}"] = a
        args.append(nc.dram_tensor(f"in_{name}", a.shape, _mybir.dt.from_np(a.dtype), kind="ExternalInput").ap())
    table = _np.zeros((PARTS, EXPERTS), dtype=_np.float32)
    for i, parts in enumerate(_PARTITIONS):
        for e, n in enumerate(parts):
            table[i, e] = n / 6
    arrays["in_part_w"] = table
    args.append(nc.dram_tensor("in_part_w", table.shape, F32, kind="ExternalInput").ap())
    out = nc.dram_tensor("out_0", (IMAGES, PLACES, D), F32, kind="ExternalOutput").ap()
    build(nc, *args, out)
    r = _run(nc, [arrays], core_ids=[0])
    return r.results[0]["out_0"]
```

```python
import concourse.bass as bass
from concourse import mybir
from contextlib import ExitStack


P = 128
F32 = mybir.dt.float32
F32R = mybir.dt.float32r
U32 = mybir.dt.uint32
I32 = mybir.dt.int32
ALU = mybir.AluOpType
ACT = mybir.ActivationFunctionType
AX = mybir.AxisListType

IMAGES, CHANNELS, SIDE, PATCH = 64, 3, 224, 16
GRID = SIDE // PATCH
PLACES = GRID * GRID
D = 128
K_PATCH = CHANNELS * PATCH * PATCH
KT = K_PATCH // P
ROWS8 = P // PATCH
HEADS, DH = 8, 64
PAIRS = HEADS // 2
EXPERTS, FF, PARTS = 6, 341, 11
FT = -(-EXPERTS * FF // P)
FPAD = FT * P
FEW = EXPERTS // 2
FT_FEW = -(-FEW * FF // P)
EPS = 1e-5
MASKED = -1000000.0
TILES = PLACES * IMAGES // P
HALF_W = GRID // 2
CHUNKS = TILES // HALF_W
BODY = 2 * HALF_W
AHEAD = 3
PACK = AHEAD + 1
BEHIND = 2
START = BEHIND + 1
TURNS = (TILES - PACK - START) // BODY
HALVES = 2
SUMS = GRID - 1
IPAIRS = IMAGES // 2
PEELED = 4
PT = 2 * PLACES
HP = PLACES // 2


class Tile:

    def __init__(self, turn, k):
        self.turn, self.k = turn, k

    def plus(self, d):
        return Tile(self.turn, self.k + d)

    def count(self, per, extra):
        return self.turn * (per * BODY) + (per * self.k + extra)

    def looped(self):
        return not isinstance(self.turn, int)

    def real(self):
        return self.looped() or 0 <= self.k < TILES


def norms(n):
    first, second = n.plus(AHEAD).real(), n.plus(-1).real()
    return slice(0 if first else 1, 2 if second else 1)


def until(eng, sem, value):
    if not isinstance(value, int) or value > 0:
        eng.wait_ge(sem, value)


def steps(eng, step):
    for n in range(-PACK, START):
        step(Tile(0, n))
    with eng.Fori(0, TURNS) as turn:
        for n in range(START, START + BODY):
            step(Tile(turn, n))
    for n in range(START + TURNS * BODY, TILES + BEHIND):
        step(Tile(0, n))


class Pair:

    def __init__(self, turn, k):
        self.turn, self.k = turn, k

    def plus(self, d):
        return Pair(self.turn, self.k + d)

    def count(self, per, extra):
        return self.turn * (2 * per) + (per * self.k + extra)

    def number(self):
        return self.k if isinstance(self.turn, int) else None

    def first(self):
        return self.number() == 0

    def last(self):
        return self.number() == IPAIRS - 1


def pairs(eng, pair):
    for k in range(PEELED):
        pair(Pair(0, k))
    with eng.Fori(0, (IPAIRS - PEELED - 2) // 2) as turn:
        for k in range(PEELED, PEELED + 2):
            pair(Pair(turn, k))
    for k in range(IPAIRS - 2, IPAIRS):
        pair(Pair(0, k))


def build(nc, x, tok_w, tok_b, wq, wkv, wo, router_w, w1, b1, w2, b2, part_w, out):
    h1_dram = nc.dram_tensor("h1_dram", (IMAGES, PLACES, D), F32, kind="Internal").ap()
    ctx = ExitStack()
    with ctx:
        def sb(name, shape, dt=F32, at=ctx):
            return at.enter_context(nc.sbuf_tensor(name, shape, dt))

        def sem(name):
            return ctx.enter_context(nc.semaphore(name))

        z2T = sb("z2T", [P, IMAGES, PLACES])
        w1_raw = sb("w1_raw", [P, FPAD])
        w2_raw = sb("w2_raw", [P, FT, D])
        ident = sb("ident", [P, P])
        b1_rows = sb("b1_rows", [FT, P])
        b1_col = sb("b1_col", [P, FT])
        b2_sb = sb("b2_sb", [EXPERTS, D])
        router_sb = sb("router_sb", [PARTS, D])
        routerT = sb("routerT", [P, PARTS])
        part_sb = sb("part_sb", [PARTS, EXPERTS])
        eps = sb("eps", [P, 1])
        onehot = sb("onehot", [EXPERTS, FPAD])
        late_expert = sb("late_expert", [EXPERTS, 1])
        places = sb("places", [IMAGES, PARTS])
        zpart = sb("zpart", [P, IMAGES, SUMS])
        zsum = sb("zsum", [P, IMAGES])

        one = ExitStack()
        xbuf = sb("xbuf", [P, 2, CHANNELS * PATCH, HALF_W * PATCH], at=one)
        patch = sb("patch", [P, 2, CHANNELS * PATCH, PATCH], at=one)
        tw_raw = sb("tw_raw", [P, K_PATCH], at=one)
        wq_raw = sb("wq_raw", [P, PAIRS, D], at=one)
        wk_raw = sb("wk_raw", [P, PAIRS, D], at=one)
        wv_raw = sb("wv_raw", [P, PAIRS, D], at=one)
        wo_raw = sb("wo_raw", [P, HEADS * DH], at=one)
        woT = sb("woT", [P, PAIRS, D], at=one)
        tok_bias = sb("tok_bias", [P, D], at=one)
        twT = sb("twT", [P, KT, D], at=one)
        qk_hi = sb("qk_hi", [P, 2, PAIRS, D], F32R, at=one)
        qk_lo = sb("qk_lo", [P, 2, PAIRS, D], F32R, at=one)
        vo = sb("vo", [P, 2, PAIRS, D], at=one)
        mask = sb("mask", [P, HEADS, IMAGES], at=one)
        xT = sb("xT", [P, HALVES, KT // 2, P], at=one)
        h0 = sb("h0", [P, HALF_W, D], at=one)
        z = sb("z", [P, 2, D], at=one)
        zT = sb("zT", [P, HALF_W, P], at=one)
        zT_hi = sb("zT_hi", [P, 2, P], F32R, at=one)
        zT_lo = sb("zT_lo", [P, 2, P], F32R, at=one)
        kq = sb("kq", [P, HEADS, 2, P], at=one)
        vw = sb("vw", [P, 2, 2, PAIRS, D], at=one)
        sm = sb("sm", [P, 2, HEADS, IMAGES], at=one)
        pe_ = sb("pe_", [P, 2, HEADS, IMAGES], at=one)
        pT = sb("pT", [P, PAIRS, P], at=one)
        h1 = sb("h1", [P, 2, D], at=one)
        z2 = sb("z2", [P, 2, D], at=one)
        smax = sb("smax", [P, 2, HEADS], at=one)
        ssum = sb("ssum", [P, 2, HEADS], at=one)
        sinv = sb("sinv", [P, 2, HEADS], at=one)
        stats = sb("stats", [P, 2, 6], at=one)
        moments = sb("moments", [P, 2, 2], at=one)
        lnv = sb("lnv", [P, 2, 1], at=one)
        guess = sb("guess", [P, 2, 1], at=one)
        newt = sb("newt", [P, 2, 2, 1], at=one)
        rstd = sb("rstd", [P, 2, 1], at=one)
        one.close()

        two = ExitStack()
        w1_hi = sb("w1_hi", [P, FPAD], F32R, at=two)
        w1_lo = sb("w1_lo", [P, FPAD], F32R, at=two)
        w2_hi = sb("w2_hi", [P, FT, D], F32R, at=two)
        w2_lo = sb("w2_lo", [P, FT, D], F32R, at=two)
        gate = sb("gate", [IMAGES, 8, 16], at=two)
        gate_idx = sb("gate_idx", [IMAGES, 8], U32, at=two)
        gateT = sb("gateT", [PARTS, IMAGES], at=two)
        ew_raw = sb("ew_raw", [EXPERTS, IMAGES], at=two)
        ew = sb("ew", [EXPERTS, IMAGES], at=two)
        ew_unit = sb("ew_unit", [P, FT, IMAGES], at=two)
        b2w = sb("b2w", [P, IMAGES], at=two)
        late_w = sb("late_w", [1, 2], at=two)
        late_used = sb("late_used", [1, 1], I32, at=two)
        ewp = sb("ewp", [P, 2, FT, 2], at=two)
        b2p = sb("b2p", [P, 2, 2], at=two)
        zp_hi = sb("zp_hi", [P, 2, PT], F32R, at=two)
        zp_lo = sb("zp_lo", [P, 2, PT], F32R, at=two)
        g = sb("g", [P, 4, PT], at=two)
        gw_hi = sb("gw_hi", [P, 4, PT], F32R, at=two)
        gw_lo = sb("gw_lo", [P, 4, PT], F32R, at=two)
        yT = sb("yT", [P, 2, PT], at=two)
        h1_in = sb("h1_in", [HP, 2, 4, D], at=two)
        o_sb = sb("o_sb", [HP, 2, 4, D], at=two)
        two.close()

        bank = [ctx.enter_context(nc.psum_tensor(f"bank{i}", [P, 512], F32)) for i in range(8)]
        xT_ps = bank[0:2]
        wide = bank[2:4]
        s_ps, t_ps, y_ps, h_ps = bank[4:8]

        tw_in, bias_in, attn_w_in, mlp_w_in = sem("tw_in"), sem("bias_in"), sem("attn_w_in"), sem("mlp_w_in")
        x_in = [sem("x_in0"), sem("x_in1")]
        consts, zeroed, prep_pe, prep_ev, prep_hi = \
            sem("consts"), sem("zeroed"), sem("prep_pe"), sem("prep_ev"), sem("prep_hi")
        packed = sem("packed")
        xT_ready, xT_done = sem("xT_ready"), sem("xT_done")
        proj_ready, h0_done = sem("proj_ready"), sem("h0_done")
        stats_done = [sem("stats1_done"), sem("stats2_done")]
        moments_done, log_done, guess_done = sem("moments_done"), sem("log_done"), sem("guess_done")
        newton = sem("newton")
        z_ready, zT_ready, zT_done, zT_lo_done = \
            sem("z_ready"), sem("zT_ready"), sem("zT_done"), sem("zT_lo_done")
        kq_ready, kq_done = sem("kq_ready"), sem("kq_done")
        vw_ready, vw_done = sem("vw_ready"), sem("vw_done")
        s_ready, masked, max_done, shifted, exp_done, sum_done, inv_done, p_ready = \
            sem("s_ready"), sem("masked"), sem("max_done"), sem("shifted"), sem("exp_done"), \
            sem("sum_done"), sem("inv_done"), sem("p_ready")
        pT_ready, pT_done, pv_ready, h1_done = sem("pT_ready"), sem("pT_done"), sem("pv_ready"), sem("h1_done")
        h1_saved = [sem("h1_saved0"), sem("h1_saved1")]
        z2_ready, z2T_ready, z2T_done = sem("z2_ready"), sem("z2T_ready"), sem("z2T_done")
        route_vec, route_pe, route_act, route_pool = \
            sem("route_vec"), sem("route_pe"), sem("route_act"), sem("route_pool")
        w_hi_done, w_lo_done = sem("w_hi_done"), sem("w_lo_done")
        row_summed, second_gate, unit_weights_done = sem("row_summed"), sem("second_gate"), sem("unit_weights_done")
        zp_hi_done, zp_ready = sem("zp_hi_done"), sem("zp_ready")
        up_ready, gelu_done, gw_hi_done, gw_ready, down_done = \
            sem("up_ready"), sem("gelu_done"), sem("gw_hi_done"), sem("gw_ready"), sem("down_done")
        late_vec, late_known, ewp_ready = sem("late_vec"), sem("late_known"), sem("ewp_ready")
        yT_done, o_ready, o_done = sem("yT_done"), sem("o_ready"), sem("o_done")
        h1_loaded = [sem("h1_loaded0"), sem("h1_loaded1")]
        o_saved = [sem("o_saved0"), sem("o_saved1")]

        block = ctx.enter_context(nc.Block())

        def load_x(eng, r, half):
            for a in range(2):
                src = x[:, :, bass.ds((2 * r + a) * PATCH, PATCH), half * HALF_W * PATCH:(half + 1) * HALF_W * PATCH]
                for c in range(CHANNELS):
                    eng.dma_start(xbuf[a * IMAGES:(a + 1) * IMAGES, half, c * PATCH:(c + 1) * PATCH, :],
                                  src[:, c, :, :]).then_inc(x_in[half], 16)
        X_DMAS = 2 * CHANNELS * 16

        def by_use(eng, mlp):
            eng.wait_ge(late_known, 1)
            used = eng.value_load(late_used[0:1, 0:1], min_val=0, max_val=1)
            with eng.If(used < 1):
                mlp(FT_FEW)
            with eng.Else():
                mlp(FT)

        @block.sync
        def _(sp):
            for dst, src in ((wq_raw, wq), (wk_raw, wkv[0:HEADS * DH, :]), (wv_raw, wkv[HEADS * DH:2 * HEADS * DH, :])):
                sp.dma_start(dst[:, :, :], src.rearrange("(t p) j -> p t j", p=P)).then_inc(attn_w_in, 16)
            sp.dma_start(wo_raw[:, :], wo).then_inc(attn_w_in, 16)
            load_x(sp, 0, 0)
            load_x(sp, 0, 1)
            sp.wait_ge(zeroed, 5)
            full = (FT - 1) * P
            rest = EXPERTS * FF - full
            sp.dma_start(w1_raw[:, 0:EXPERTS * FF].rearrange("p (e f) -> p e f", e=EXPERTS),
                          w1.rearrange("e d f -> d e f")).then_inc(mlp_w_in, 16)
            w2_rows = w2.rearrange("e f d -> (e f) d")
            sp.dma_start(w2_raw[:, 0:FT - 1, :], w2_rows[0:full, :].rearrange("(t p) d -> p t d", p=P)).then_inc(mlp_w_in, 16)
            sp.dma_start(w2_raw[0:rest, FT - 1, :], w2_rows[full:full + rest, :]).then_inc(mlp_w_in, 16)
            b1_flat = b1.rearrange("e f -> (e f)")
            sp.dma_start(b1_rows[0:FT - 1, :], b1_flat[0:full].rearrange("(t p) -> t p", p=P)).then_inc(mlp_w_in, 16)
            sp.dma_start(b1_rows[FT - 1:FT, 0:rest], b1_flat[full:full + rest].rearrange("(o p) -> o p", o=1)).then_inc(mlp_w_in, 16)
            sp.dma_start(b2_sb[:, :], b2).then_inc(mlp_w_in, 16)
            sp.dma_start(router_sb[:, :], router_w).then_inc(mlp_w_in, 16)
            sp.dma_start(part_sb[:, :], part_w).then_inc(mlp_w_in, 16)


            def save_h1(m):
                sp.wait_ge(h1_done, m.count(1, 1))
                r2 = m.k // GRID * 2
                w = m.k % GRID
                for a in range(2):
                    place = m.turn * (2 * GRID) + ((r2 + a) * GRID + w)
                    sp.dma_start(h1_dram[:, bass.ds(place, 1), :].rearrange("b o d -> b (o d)"),
                                 h1[a * IMAGES:(a + 1) * IMAGES, m.k % 2, :]).then_inc(h1_saved[m.k % 2], 16)

            def step(n):
                m = n.plus(AHEAD)
                if m.real() and m.k % HALF_W == HALF_W - 1 and (m.looped() or m.k + BODY < TILES):
                    sp.wait_ge(packed, m.count(2, 2))
                    load_x(sp, m.turn + (m.k // BODY + 1), m.k // HALF_W % 2)
                if n.plus(-1).real():
                    save_h1(n.plus(-1))

            steps(sp, step)
            for k in range(2):
                sp.wait_ge(h1_saved[k], 32 * TILES // 2)

            def load_h1(j):
                if j.number() not in (0, 1):
                    sp.wait_ge(o_done, j.count(1, -1))
                for b in range(2):
                    img = j.count(2, b)
                    sp.dma_start(h1_in[:, j.k % 2, 2 * b:2 * b + 2, :],
                                 h1_dram[bass.ds(img, 1), :, :].rearrange("o (p a) d -> (o p) a d", a=2)
                                 ).then_inc(h1_loaded[j.k % 2], 16)

            def save(j):
                sp.wait_ge(o_done, j.count(1, 1))
                for b in range(2):
                    img = j.count(2, b)
                    sp.dma_start(out[bass.ds(img, 1), :, :].rearrange("o (p a) d -> (o p) a d", a=2),
                                 o_sb[:, j.k % 2, 2 * b:2 * b + 2, :]).then_inc(o_saved[j.k % 2], 16)

            def pair(j):
                load_h1(j)
                if not j.first():
                    save(j.plus(-1))
                if j.last():
                    save(j)
            pairs(sp, pair)
            for k in range(2):
                sp.wait_ge(o_saved[k], 32 * IPAIRS // 2)

        @block.gpsimd
        def _(pool):
            pool.memset(ident[:, :], 0.0).then_inc(zeroed, 1)
            pool.memset(mask[:, :, :], 3.0e38).then_inc(zeroed, 1)
            pool.memset(eps[:, :], EPS).then_inc(consts, 1)
            pool.memset(b1_rows[:, :], 0.0).then_inc(zeroed, 1)
            pool.memset(w1_raw[:, EXPERTS * FF:FPAD], 0.0).then_inc(zeroed, 1)
            pool.memset(w2_raw[:, FT - 1, :], 0.0).then_inc(zeroed, 1)
            pool.wait_ge(zeroed, 5)
            pool.affine_select(out=ident[:, :], in_=ident[:, :], compare_op=ALU.not_equal, fill=1.0,
                               base=0, pattern=[[-1, P]], channel_multiplier=1).then_inc(consts, 1)
            for a in range(2):
                pool.wait_ge(consts, 2 + a)
                m = mask[a * IMAGES:(a + 1) * IMAGES, :, :]
                pool.affine_select(out=m, in_=m, compare_op=ALU.is_ge, fill=MASKED, base=0,
                                   pattern=[[0, HEADS], [-1, IMAGES]], channel_multiplier=1).then_inc(consts, 1)

            pool.wait_ge(consts, 4)

            pool.memset(onehot[:, :], 1.0).then_inc(route_pool, 1)
            pool.iota(places[:, :], pattern=[[1, PARTS]], base=0, channel_multiplier=0,
                      allow_small_or_imprecise_dtypes=True).then_inc(route_pool, 1)
            pool.wait_ge(route_pool, 2)
            pool.affine_select(out=onehot[:, :], in_=onehot[:, :], compare_op=ALU.is_ge, fill=0.0, base=0,
                               pattern=[[1, FPAD]], channel_multiplier=-FF).then_inc(route_pool, 1)
            pool.wait_ge(route_pool, 3)
            pool.affine_select(out=onehot[:, :], in_=onehot[:, :], compare_op=ALU.is_ge, fill=0.0, base=FF - 1,
                               pattern=[[-1, FPAD]], channel_multiplier=FF).then_inc(route_pool, 1)
            pool.memset(late_expert[:, :], 1.0).then_inc(route_pool, 1)
            pool.wait_ge(route_pool, 5)
            pool.affine_select(out=late_expert[:, :], in_=late_expert[:, :], compare_op=ALU.is_ge, fill=0.0,
                               base=-FEW, pattern=[[0, 1]], channel_multiplier=1).then_inc(route_pool, 1)

            def step(n):
                b = n.k % 2
                if n.real():
                    pool.wait_ge(max_done, n.count(1, 1))
                    pool.tensor_tensor(sm[:, b, :, :], sm[:, b, :, :],
                                       smax[:, b, :].unsqueeze(2).to_broadcast([P, HEADS, IMAGES]),
                                       ALU.subtract).then_inc(shifted, 1)
                if n.real():
                    pool.wait_ge(inv_done, n.count(1, 1))
                    pool.tensor_tensor(pe_[:, b, :, :], pe_[:, b, :, :],
                                       sinv[:, b, :].unsqueeze(2).to_broadcast([P, HEADS, IMAGES]),
                                       ALU.mult).then_inc(p_ready, 1)
            steps(pool, step)

            pool.wait_ge(w_hi_done, 1)
            pool.tensor_tensor(w1_lo[:, :], w1_raw[:, :], w1_hi[:, :].bitcast(F32), ALU.subtract).then_inc(w_lo_done, 1)
            pool.wait_ge(w_hi_done, 2)
            pool.tensor_tensor(w2_lo[:, :, :], w2_raw[:, :, :], w2_hi[:, :, :].bitcast(F32), ALU.subtract).then_inc(w_lo_done, 1)

            pool.wait_ge(z2T_done, TILES)
            for k in range(2):
                pool.wait_ge(h1_saved[k], 32 * TILES // 2)

            def mlp(tiles):
                def weigh(j, t):
                    pool.wait_ge(gelu_done, j.count(tiles, t + 1))
                    if not (j.first() and t < 4):
                        pool.wait_ge(down_done, j.count(tiles, t - 3))
                    if t == 0:
                        pool.wait_ge(ewp_ready, j.count(1, 1))
                    pool.tensor_tensor(gw_hi[:, t % 4, :].rearrange("p (b s) -> p b s", b=2),
                                       g[:, t % 4, :].rearrange("p (b s) -> p b s", b=2),
                                       ewp[:, j.k % 2, t, :].unsqueeze(2).to_broadcast([P, 2, PLACES]),
                                       ALU.mult).then_inc(gw_hi_done, 1)

                def pair(j):
                    for t in range(tiles):
                        weigh(j, t)
                pairs(pool, pair)

            by_use(pool, mlp)

        @block.scalar
        def _(act):
            act.dma_start(tw_raw[:, :], tok_w).then_inc(tw_in, 16)
            act.dma_start(tok_bias[:, :], tok_b.partition_broadcast(P)).then_inc(bias_in, 16)
            nc.scalar.preload_act_table_set("natural_log_exp_and_others")
            for i in range(2):
                act.wait_ge(prep_pe, i + 1)
                act.activation(twT[:, 3 * i:3 * i + 3, :], bank[i][:, 0:3 * P].rearrange("p (k e) -> p k e", e=D),
                               ACT.Copy).then_inc(prep_ev, 1)
            for q in range(2):
                act.wait_ge(prep_pe, 4 + q)
                act.activation(qk_hi[:, q, :, :], bank[4 + q][:, :].rearrange("p (k e) -> p k e", e=D),
                               ACT.Copy, scale=DH ** -0.5).then_inc(prep_hi, 1)

            def guess_rstd(n):
                w = norms(n)
                act.wait_ge(moments_done, n.count(1, AHEAD + 1))
                act.activation(lnv[:, w, :], moments[:, w, 1:2], ACT.Ln, bias=eps[:, 0:1]).then_inc(log_done, 1)
                act.wait_ge(log_done, n.count(1, AHEAD + 1))
                act.activation(guess[:, w, :], lnv[:, w, :], ACT.Exp, scale=-0.5).then_inc(guess_done, 1)

            def take_x(m, h):
                act.wait_ge(xT_ready, m.count(2, h + 1))
                until(act, proj_ready, m.count(1, 0))
                act.activation(xT[:, h, :, :], xT_ps[h][:, 0:3 * P].rearrange("p (k t) -> p k t", t=P),
                               ACT.Copy).then_inc(xT_done, 1)

            def take_vw(n, a):
                act.wait_ge(vw_ready, n.count(2, a + 1))
                if a == 0:
                    until(act, pv_ready, n.count(1, -1))
                act.activation(vw[:, n.k % 2, a, :, :], wide[a][:, :].rearrange("p (t f) -> p t f", f=D),
                               ACT.Copy).then_inc(vw_done, 1)

            def take_kq(m, i):
                act.wait_ge(kq_ready, m.count(2, i + 1))
                if i == 0:
                    until(act, s_ready, m.count(1, 0))
                act.activation(kq[:, 2 * i:2 * i + 2, :, :],
                               wide[i % 2][:, :].rearrange("p (h a t) -> p h a t", a=2, t=P),
                               ACT.Copy).then_inc(kq_done, 1)

            act.wait_ge(consts, 1)

            def step(n):
                emb, nrm, key, prev, last = n.plus(AHEAD), n.plus(2), n.plus(1), n.plus(-1), n.plus(-BEHIND)
                pair_due = n.k % 2 == 1 and key.real()
                norm_due = nrm.real() or last.real()
                if norm_due and n.k % 2 == 0:
                    guess_rstd(n.plus(-1))
                if emb.real():
                    take_x(emb, 0)
                if emb.real() and n.k % 2 == 0:
                    take_x(emb, 1)
                if norm_due and n.k % 2 == 1:
                    guess_rstd(n.plus(-1))
                if n.real():
                    take_vw(n, 0)
                if emb.real() and n.k % 2 == 1:
                    take_x(emb, 1)
                if nrm.real():
                    act.wait_ge(zT_ready, nrm.count(1, 1))
                    act.activation(zT_hi[:, nrm.k % 2, :], y_ps[:, 0:P], ACT.Copy)
                    act.activation(zT[:, nrm.k % HALF_W, :], y_ps[:, 0:P], ACT.Copy).then_inc(zT_done, 1)
                if prev.real():
                    act.wait_ge(pT_ready, prev.count(1, 1))
                    act.activation(pT[:, :, :], t_ps[:, :].rearrange("p (t q) -> p t q", q=P), ACT.Copy).then_inc(pT_done, 1)
                if n.real():
                    act.wait_ge(shifted, n.count(1, 1))
                    act.activation(pe_[:, n.k % 2, :, :], sm[:, n.k % 2, :, :], ACT.Exp).then_inc(exp_done, 1)
                    take_vw(n, 1)
                if pair_due:
                    for i in range(PAIRS):
                        take_kq(key, i)
                if last.real():
                    act.wait_ge(z2T_ready, last.count(1, 1))
                    w0 = last.turn * (2 * GRID) + (last.k // GRID * 2 * GRID + last.k % GRID)
                    for a in range(2):
                        act.activation(z2T[:, :, bass.ds(w0 + a * GRID, 1)].rearrange("p b o -> p (b o)"),
                                       h_ps[:, a * IMAGES:(a + 1) * IMAGES], ACT.Copy).then_inc(z2T_done, 1)
            def step_and_split(n):
                step(n)
                if not n.looped() and n.k == TILES - 3:
                    act.wait_ge(mlp_w_in, 8 * 16)
                    act.wait_ge(packed, 2 * TILES)
                    act.activation(w1_hi[:, :], w1_raw[:, :], ACT.Copy).then_inc(w_hi_done, 1)
                if not n.looped() and n.k == TILES - 2:
                    act.activation(w2_hi[:, :, :], w2_raw[:, :, :], ACT.Copy).then_inc(w_hi_done, 1)
            steps(act, step_and_split)

            act.wait_ge(p_ready, TILES)
            act.wait_ge(h1_saved[0], 32 * TILES // 2)
            act.wait_ge(h1_saved[1], 32 * TILES // 2)
            act.wait_ge(z2T_done, 2 * TILES)
            act.activation(zp_hi[:, 0, :], z2T[:, 0:2, :].rearrange("p b t -> p (b t)"), ACT.Copy).then_inc(zp_hi_done, 1)
            act.wait_ge(route_vec, 3)
            act.activation(gate[:, 1, 0:PARTS], gate[:, 0, 0:PARTS], ACT.Exp, bias=gate[:, 2, 8:9]).then_inc(route_act, 1)

            def mlp(tiles):
                def gelu(j, t):
                    act.wait_ge(up_ready, j.count(tiles, t + 1))
                    if not (j.first() and t < 4):
                        act.wait_ge(gw_ready, j.count(tiles, t - 3))
                    act.activation(g[:, t % 4, :], bank[t % 4][:, 0:PT], ACT.Gelu,
                                   bias=b1_col[:, t:t + 1]).then_inc(gelu_done, 1)

                def split_z(j):
                    until(act, up_ready, j.count(tiles, -tiles))
                    act.activation(zp_hi[:, j.k % 2, :],
                                   z2T[:, bass.ds(j.count(2, 0), 2), :].rearrange("p b t -> p (b t)"),
                                   ACT.Copy).then_inc(zp_hi_done, 1)

                def take_y(j):
                    act.wait_ge(down_done, j.count(tiles, tiles))
                    if not j.first():
                        act.wait_ge(o_ready, j.count(1, 0))
                    for b in range(2):
                        act.activation(yT[:, j.k % 2, b * PLACES:(b + 1) * PLACES],
                                       bank[4 + j.k % 2][:, b * PLACES:(b + 1) * PLACES], ACT.Identity,
                                       bias=b2p[:, j.k % 2, b:b + 1]).then_inc(yT_done, 1)

                def pair(j):
                    for t in range(tiles):
                        gelu(j, t)
                        if t == 1 and not j.last():
                            split_z(j.plus(1))
                        if t == 3 and not j.first():
                            take_y(j.plus(-1))
                    if j.last():
                        take_y(j)
                pairs(act, pair)

            act.wait_ge(prep_ev, 9)
            by_use(act, mlp)

        @block.tensor
        def _(pe):
            def mm3(o, a_hi, a_lo, b_hi, b_lo, start, stop):
                pe.matmul(o, a_hi, b_hi, start=start, stop=False)
                pe.matmul(o, a_lo, b_hi, start=False, stop=False)
                return pe.matmul(o, a_hi, b_lo, start=False, stop=stop)

            pe.wait_ge(consts, 4)
            pe.wait_ge(tw_in, 16)
            for i in range(2):
                for k in range(3):
                    mm = pe.transpose(bank[i][:, k * P:(k + 1) * P], tw_raw[:, (3 * i + k) * P:(3 * i + k + 1) * P], ident[:, :])
                mm.then_inc(prep_pe, 1)
            pe.wait_ge(attn_w_in, 4 * 16)
            for t in range(PAIRS):
                mm = pe.transpose(bank[2][:, t * P:(t + 1) * P], wo_raw[:, t * P:(t + 1) * P], ident[:, :])
            mm.then_inc(prep_pe, 1)
            for q in range(2):
                for t in range(PAIRS):
                    r = slice(q * DH, (q + 1) * DH)
                    mm = pe.matmul(bank[4 + q][:, t * P:(t + 1) * P], wk_raw[r, t, :], wq_raw[r, t, :], start=True, stop=True)
                mm.then_inc(prep_pe, 1)
            pe.wait_ge(prep_ev, 5)
            for q in range(2):
                for t in range(PAIRS):
                    r = slice(q * DH, (q + 1) * DH)
                    mm = pe.matmul(bank[6 + q][:, t * P:(t + 1) * P], wv_raw[r, t, :], woT[r, t, :], start=True, stop=True)
                mm.then_inc(prep_pe, 1)
            pe.wait_ge(prep_ev, 7)

            def turn_x(m, h):
                pe.wait_ge(packed, m.count(2, h + 1))
                until(pe, xT_done, m.count(2, h - 1))
                for k in range(3):
                    row = (3 * h + k) * ROWS8
                    mm = pe.transpose(xT_ps[h][:, k * P:(k + 1) * P],
                                      patch[:, m.k % 2, row:row + ROWS8, :].rearrange("p r c -> p (r c)"), ident[:, :])
                mm.then_inc(xT_ready, 1)

            def project(m, h):
                pe.wait_ge(xT_done, m.count(2, h + 1))
                if h == 0:
                    until(pe, h0_done, m.count(1, 0))
                    until(pe, z2T_done, m.count(2, -2 * 5))
                for k in range(h * KT // 2, (h + 1) * KT // 2):
                    mm = pe.matmul(h_ps[:, 0:D], xT[:, h, k % 3, :], twT[:, k, :], start=(k == 0), stop=(k == KT - 1))
                if h == 1:
                    mm.then_inc(proj_ready, 1)

            def turn_z(m):
                pe.wait_ge(z_ready, m.count(1, 1))
                until(pe, h1_done, m.count(1, -3))
                pe.transpose(y_ps[:, 0:P], z[:, m.k % 2, :], ident[:, :]).then_inc(zT_ready, 1)

            def keys(m, i):
                if i == 0:
                    pe.wait_ge(zT_lo_done, m.count(1, 2))
                if i < 2:
                    if m.looped() or m.k > 0:
                        pe.wait_ge(vw_done, m.count(2, i - 1))
                else:
                    pe.wait_ge(kq_done, m.count(2, i - 1))
                for q in range(2):
                    mm = mm3(wide[i % 2][:, q * 2 * P:(q + 1) * 2 * P], qk_hi[:, q, i, :], qk_lo[:, q, i, :],
                             zT_hi[:, :, :].rearrange("p a t -> p (a t)"), zT_lo[:, :, :].rearrange("p a t -> p (a t)"),
                             True, True)
                mm.then_inc(kq_ready, 1)

            def values(n, a):
                if n.k % 2 == 0:
                    pe.wait_ge(kq_done, n.count(2, a + 3))
                else:
                    pe.wait_ge(vw_done, n.count(2, a - 1))
                lhs = zT[:, n.k % HALF_W, a * IMAGES:(a + 1) * IMAGES]
                for q in range(2):
                    mm = pe.matmul(wide[a][q * IMAGES:(q + 1) * IMAGES, :], lhs, vo[:, q, :, :], start=True, stop=True)
                mm.then_inc(vw_ready, 1)

            def scores(n):
                pe.wait_ge(kq_done, n.count(2, 4 - n.k % 2 * 2))
                until(pe, masked, n.count(1, 0))
                for a in range(2):
                    t = slice(a * IMAGES, (a + 1) * IMAGES)
                    mm = pe.matmul(s_ps[t, :], zT[:, n.k % HALF_W, t], kq[:, :, n.k % 2, t], start=True, stop=True)
                mm.then_inc(s_ready, 1)

            def turn_p(m):
                pe.wait_ge(p_ready, m.count(1, 1))
                until(pe, pT_done, m.count(1, 0))
                for t in range(PAIRS):
                    mm = pe.transpose(t_ps[:, t * P:(t + 1) * P], pe_[:, m.k % 2, 2 * t:2 * t + 2, :].rearrange("p h k -> p (h k)"), ident[:, :])
                mm.then_inc(pT_ready, 1)

            def mix(m, h):
                if h == 0:
                    pe.wait_ge(pT_done, m.count(1, 1))
                    pe.wait_ge(vw_done, m.count(2, 2))
                    until(pe, h1_done, m.count(1, 0))
                    pe.wait_ge(zT_done, m.count(1, 4) if m.looped() else min(m.k + 4, TILES))
                for t in range(h * PAIRS // 2, (h + 1) * PAIRS // 2):
                    for a in range(2):
                        s = slice(a * IMAGES, (a + 1) * IMAGES)
                        mm = pe.matmul(y_ps[s, 0:D], pT[:, t, s], vw[:, m.k % 2, a, t, :],
                                       start=(t == 0), stop=(t == PAIRS - 1))
                if h == 1:
                    mm.then_inc(pv_ready, 1)

            def turn_z2(m):
                pe.wait_ge(z2_ready, m.count(1, 1))
                h0_seen = m.count(1, 6) if m.looped() else min(m.k + 6, TILES)
                pe.wait_ge(h0_done, h0_seen)
                pe.transpose(h_ps[:, 0:P], z2[:, m.k % 2, :], ident[:, :]).then_inc(z2T_ready, 1)

            def step(n):
                emb, nrm, key, prev, last = n.plus(AHEAD), n.plus(2), n.plus(1), n.plus(-1), n.plus(-BEHIND)
                if emb.real():
                    turn_x(emb, 0)
                if emb.real() and n.k % 2 == 0:
                    turn_x(emb, 1)
                if n.real():
                    scores(n)
                    values(n, 0)
                if emb.real() and n.k % 2 == 1:
                    turn_x(emb, 1)
                if n.real():
                    values(n, 1)
                if prev.real():
                    turn_p(prev)
                if nrm.real():
                    turn_z(nrm)
                if emb.real():
                    project(emb, 0)
                if emb.real():
                    project(emb, 1)
                pair_due = n.k % 2 == 1 and key.real()
                if pair_due:
                    keys(key, 0)
                if prev.real():
                    mix(prev, 0)
                if pair_due:
                    keys(key, 1)
                if prev.real():
                    mix(prev, 1)
                if pair_due:
                    keys(key, 2)
                    keys(key, 3)
                if last.real():
                    turn_z2(last)
            steps(pe, step)

            pe.wait_ge(mlp_w_in, 8 * 16)
            pe.wait_ge(vw_done, 2 * TILES)
            pe.transpose(bank[3][:, 0:FT], b1_rows[:, :], ident[0:FT, 0:FT])
            pe.transpose(bank[3][:, 64:64 + PARTS], router_sb[:, :], ident[0:PARTS, 0:PARTS]).then_inc(prep_pe, 1)

            pe.wait_ge(prep_ev, 9)
            pe.wait_ge(route_vec, 1)
            pe.wait_ge(z2T_done, 2 * TILES)
            pe.matmul(bank[6][0:IMAGES, 0:PARTS], zsum[:, :], routerT[:, :], start=True, stop=True).then_inc(route_pe, 1)
            pe.wait_ge(route_vec, 13)
            pe.transpose(bank[6][0:PARTS, 0:IMAGES], gate[:, 7, 0:PARTS], ident[0:IMAGES, 0:IMAGES]).then_inc(route_pe, 1)
            pe.wait_ge(route_vec, 14)
            pe.matmul(bank[6][0:EXPERTS, 0:IMAGES], part_sb[:, :], gateT[:, :], start=True, stop=True).then_inc(route_pe, 1)
            pe.wait_ge(route_vec, 16)
            pe.wait_ge(route_pool, 6)
            pe.matmul(bank[7][0:1, 0:IMAGES], late_expert[:, :], ew[:, :], start=True, stop=True).then_inc(route_pe, 1)

            def unit_weights(first, end):
                for t in range(first, end):
                    mm = pe.matmul(bank[4 + t // 8][:, t % 8 * IMAGES:(t % 8 + 1) * IMAGES],
                                   onehot[:, t * P:(t + 1) * P], ew[:, :], start=True, stop=True)
                return mm

            unit_weights(0, FT_FEW)
            pe.matmul(bank[6][:, 0:IMAGES], b2_sb[:, :], ew[:, :], start=True, stop=True).then_inc(route_pe, 1)
            pe.wait_ge(w_lo_done, 1)

            def mlp(tiles):
                def up(j, t):
                    if t == 0:
                        pe.wait_ge(zp_ready, j.count(1, 1))
                    if not (j.first() and t < 4):
                        pe.wait_ge(gelu_done, j.count(tiles, t - 3))
                    f = slice(t * P, (t + 1) * P)
                    mm3(bank[t % 4][:, 0:PT], w1_hi[:, f], w1_lo[:, f], zp_hi[:, j.k % 2, :], zp_lo[:, j.k % 2, :],
                        True, True).then_inc(up_ready, 1)

                def down(j, t):
                    pe.wait_ge(gw_ready, j.count(tiles, t + 1))
                    if t == 0 and j.number() not in (0, 1):
                        pe.wait_ge(yT_done, j.count(2, -2))
                    mm = mm3(bank[4 + j.k % 2][:, 0:PT], w2_hi[:, t, :], w2_lo[:, t, :], gw_hi[:, t % 4, :],
                             gw_lo[:, t % 4, :], t == 0, t == tiles - 1)
                    mm.then_inc(down_done, 1)
                    return mm

                def turn_y(j):
                    pe.wait_ge(yT_done, j.count(2, 2))
                    if not j.first():
                        pe.wait_ge(o_done, j.count(1, 0))
                    for b in range(2):
                        for a in range(2):
                            c = 2 * b + a
                            mm = pe.transpose(bank[6][0:HP, c * D:(c + 1) * D],
                                              yT[:, j.k % 2, b * PLACES + a:(b + 1) * PLACES:2], ident[:, :])
                    mm.then_inc(o_ready, 1)

                lead = 3
                for t in range(lead):
                    up(Pair(0, 0), t)
                if tiles > FT_FEW:
                    unit_weights(FT_FEW, tiles).then_inc(route_pe, 1)
                pe.wait_ge(w_lo_done, 2)

                def pair(j):
                    for t in range(tiles):
                        if t + lead < tiles:
                            up(j, t + lead)
                        elif not j.last():
                            up(j.plus(1), t + lead - tiles)
                        down(j, t)
                        if t == 5 and not j.first():
                            turn_y(j.plus(-1))
                    if j.last():
                        turn_y(j)
                pairs(pe, pair)

            by_use(pe, mlp)

        @block.vector
        def _(dve):
            dve.wait_ge(prep_pe, 3)
            dve.tensor_copy(woT[:, :, :], bank[2][:, :].rearrange("p (t f) -> p t f", f=D)).then_inc(prep_ev, 1)
            for q in range(2):
                dve.wait_ge(prep_hi, 1 + q)
                dve.scalar_tensor_tensor(out=qk_lo[:, q, :, :], in0=bank[4 + q][:, :].rearrange("p (k e) -> p k e", e=D),
                                         scalar=DH ** -0.5, in1=qk_hi[:, q, :, :].bitcast(F32), op0=ALU.mult,
                                         op1=ALU.subtract).then_inc(prep_ev, 1)
            for q in range(2):
                dve.wait_ge(prep_pe, 6 + q)
                dve.tensor_copy(vo[:, q, :, :], bank[6 + q][:, :].rearrange("p (t f) -> p t f", f=D)).then_inc(prep_ev, 1)
            dve.wait_ge(bias_in, 16)
            dve.wait_ge(consts, 4)

            def newton_step(n):
                w = norms(n)
                y = guess[:, w, :]
                dve.wait_ge(guess_done, n.count(1, AHEAD + 1))
                dve.scalar_tensor_tensor(out=newt[:, w, 0, :], in0=moments[:, w, 1:2], scalar=EPS, in1=y,
                                         op0=ALU.add, op1=ALU.mult).then_inc(newton, 1)
                dve.wait_ge(newton, n.count(3, 3 * AHEAD + 1))
                dve.scalar_tensor_tensor(out=newt[:, w, 1, :], in0=newt[:, w, 0, :], scalar=-0.5, in1=y,
                                         op0=ALU.mult, op1=ALU.mult).then_inc(newton, 1)
                dve.wait_ge(newton, n.count(3, 3 * AHEAD + 2))
                dve.scalar_tensor_tensor(out=rstd[:, w, :], in0=newt[:, w, 1, :], scalar=1.5, in1=y,
                                         op0=ALU.add, op1=ALU.mult).then_inc(newton, 1)
                dve.wait_ge(newton, n.count(3, 3 * AHEAD + 3))

            def norm_apply(which, src, dst, done):
                dve.tensor_scalar(dst, src, moments[:, which, 0:1], rstd[:, which, 0:1], ALU.subtract, ALU.mult).then_inc(done, 1)

            def pack(m, h):
                c, w = m.k // HALF_W % 2, m.k % HALF_W
                rows = slice(h * CHANNELS * PATCH // 2, (h + 1) * CHANNELS * PATCH // 2)
                if h == 0:
                    if w == 0:
                        dve.wait_ge(x_in[c], m.turn * X_DMAS + X_DMAS * (m.k // BODY + 1))
                    until(dve, xT_ready, m.count(2, -2))
                dve.tensor_copy(patch[:, m.k % 2, rows, :], xbuf[:, c, rows, w * PATCH:(w + 1) * PATCH]).then_inc(packed, 1)

            def finish_norms(n):
                nrm, last = n.plus(AHEAD - 1), n.plus(-BEHIND)
                if nrm.real() or last.real():
                    newton_step(n.plus(-1))
                if nrm.real():
                    norm_apply(0, h0[:, nrm.k % HALF_W, :], z[:, nrm.k % 2, :], z_ready)
                if last.real():
                    norm_apply(1, h1[:, last.k % 2, :], z2[:, last.k % 2, :], z2_ready)

            def step(n):
                emb, nrm, prev, last = n.plus(AHEAD), n.plus(AHEAD - 1), n.plus(-1), n.plus(-BEHIND)
                b = n.k % 2
                if n.k % 2 == 0:
                    finish_norms(n)
                if n.real():
                    dve.wait_ge(s_ready, n.count(1, 1))
                    until(dve, exp_done, n.count(1, -1))
                    dve.tensor_tensor(sm[:, b, :, :], s_ps[:, :].rearrange("p (h k) -> p h k", k=IMAGES),
                                      mask[:, :, :], ALU.min).then_inc(masked, 1)
                    dve.wait_ge(masked, n.count(1, 1))
                    dve.tensor_reduce(smax[:, b, :], sm[:, b, :, :], AX.X, ALU.max).then_inc(max_done, 1)
                if n.k % 2 == 1:
                    finish_norms(n)
                if nrm.real():
                    dve.wait_ge(zT_done, nrm.count(1, 1))
                    dve.tensor_tensor(zT_lo[:, nrm.k % 2, :], zT[:, nrm.k % HALF_W, :],
                                      zT_hi[:, nrm.k % 2, :].bitcast(F32), ALU.subtract).then_inc(zT_lo_done, 1)
                if n.plus(PACK).real():
                    pack(n.plus(PACK), 0)
                if emb.real():
                    dve.wait_ge(proj_ready, emb.count(1, 1))
                    dve.tensor_tensor(h0[:, emb.k % HALF_W, :], h_ps[:, 0:D], tok_bias[:, :], ALU.add).then_inc(h0_done, 1)
                if n.real():
                    dve.wait_ge(exp_done, n.count(1, 1))
                    dve.tensor_reduce(ssum[:, b, :], pe_[:, b, :, :], AX.X, ALU.add).then_inc(sum_done, 1)
                    dve.wait_ge(sum_done, n.count(1, 1))
                    dve.reciprocal(sinv[:, b, :], ssum[:, b, :]).then_inc(inv_done, 1)
                if emb.real():
                    dve.wait_ge(h0_done, emb.count(1, 1))
                    dve.bn_stats(stats[:, 0, :], h0[:, emb.k % HALF_W, :]).then_inc(stats_done[0], 1)
                if prev.real():
                    dve.wait_ge(pv_ready, prev.count(1, 1))
                    until(dve, h1_saved[prev.k % 2], prev.turn * (16 * BODY) + 32 * (prev.k // 2))
                    dve.tensor_tensor(h1[:, prev.k % 2, :], y_ps[:, 0:D], h0[:, prev.k % HALF_W, :], ALU.add).then_inc(h1_done, 1)
                    dve.wait_ge(h1_done, prev.count(1, 1))
                    dve.bn_stats(stats[:, 1, :], h1[:, prev.k % 2, :]).then_inc(stats_done[1], 1)
                if emb.real():
                    dve.wait_ge(stats_done[0], emb.count(1, 1))
                if prev.real():
                    dve.wait_ge(stats_done[1], prev.count(1, 1))
                if n.plus(PACK).real():
                    pack(n.plus(PACK), 1)
                for which, tile in ((0, emb), (1, prev)):
                    if tile.real():
                        mom = dve.bn_aggr(moments[:, which, :], stats[:, which, :])
                if emb.real() or prev.real():
                    mom.then_inc(moments_done, 1)
            def sum_row(c):
                span = slice(c * GRID, PLACES if c == SUMS - 1 else (c + 1) * GRID)
                return dve.tensor_reduce(zpart[:, :, c], z2T[:, :, span], AX.X, ALU.add)

            def step_and_sum(n):
                step(n)
                c = n.k - START - TURNS * BODY
                if not n.looped() and 0 <= c < SUMS - 1:
                    dve.wait_ge(z2T_done, 2 * BODY * (c // 2 + 1))
                    sum_row(c).then_inc(row_summed, 1)
            steps(dve, step_and_sum)

            rv = [0]

            def link(ins):
                rv[0] += 1
                ins.then_inc(route_vec, 1)

            dve.wait_ge(prep_pe, 8)
            dve.tensor_copy(b1_col[:, :], bank[3][:, 0:FT]).then_inc(prep_ev, 1)
            dve.tensor_copy(routerT[:, :], bank[3][:, 64:64 + PARTS]).then_inc(prep_ev, 1)
            dve.wait_ge(z2T_done, 2 * TILES)
            dve.wait_ge(p_ready, TILES)
            dve.wait_ge(h1_saved[0], 32 * TILES // 2)
            dve.wait_ge(h1_saved[1], 32 * TILES // 2)
            sum_row(SUMS - 1).then_inc(row_summed, 1)
            dve.wait_ge(row_summed, SUMS)
            link(dve.tensor_reduce(zsum[:, :], zpart[:, :, :], AX.X, ALU.add))
            dve.wait_ge(route_pe, 1)
            link(dve.tensor_scalar(gate[:, 0, 0:PARTS], bank[6][0:IMAGES, 0:PARTS], 1.0 / PLACES, None, ALU.mult))
            dve.wait_ge(route_vec, 2)
            link(dve.tensor_reduce(gate[:, 2, 8:9], gate[:, 0, 0:PARTS], AX.X, ALU.max, negate=True))
            dve.wait_ge(route_act, 1)
            link(dve.tensor_reduce(gate[:, 2, 9:10], gate[:, 1, 0:PARTS], AX.X, ALU.add))
            dve.wait_ge(route_vec, 4)
            link(dve.reciprocal(gate[:, 2, 10:11], gate[:, 2, 9:10]))
            dve.wait_ge(route_vec, 5)
            link(dve.tensor_scalar(gate[:, 3, 0:PARTS], gate[:, 1, 0:PARTS], gate[:, 2, 10:11], None, ALU.mult))
            dve.wait_ge(route_vec, 6)
            link(dve.max(gate[:, 4, 0:8], gate[:, 3, 0:PARTS]))
            dve.wait_ge(route_vec, 7)
            link(dve.max_index(gate_idx[:, :], gate[:, 4, 0:8], gate[:, 3, 0:PARTS]))
            link(dve.tensor_tensor(gate[:, 2, 11:12], gate[:, 4, 0:1], gate[:, 4, 1:2], ALU.add))
            dve.wait_ge(route_vec, 9)
            link(dve.reciprocal(gate[:, 2, 12:13], gate[:, 2, 11:12]))
            link(dve.tensor_copy(gate[:, 2, 14:16], gate_idx[:, 0:2]))
            dve.wait_ge(route_vec, 11)
            dve.wait_ge(route_pool, 2)
            link(dve.tensor_scalar(gate[:, 5, 0:PARTS], places[:, :], gate[:, 2, 14:15], gate[:, 4, 0:1], ALU.is_equal, ALU.mult))
            dve.tensor_scalar(gate[:, 6, 0:PARTS], places[:, :], gate[:, 2, 15:16], gate[:, 4, 1:2],
                              ALU.is_equal, ALU.mult).then_inc(second_gate, 1)
            dve.wait_ge(route_vec, 12)
            dve.wait_ge(second_gate, 1)
            dve.tensor_tensor(gate[:, 7, 0:PARTS], gate[:, 5, 0:PARTS], gate[:, 6, 0:PARTS], ALU.add).then_inc(second_gate, 1)
            dve.wait_ge(second_gate, 2)
            link(dve.tensor_scalar(gate[:, 7, 0:PARTS], gate[:, 7, 0:PARTS], gate[:, 2, 12:13], None, ALU.mult))
            dve.wait_ge(route_pe, 2)
            link(dve.tensor_copy(gateT[:, :], bank[6][0:PARTS, 0:IMAGES]))
            dve.wait_ge(route_pe, 3)
            link(dve.tensor_copy(ew_raw[:, :], bank[6][0:EXPERTS, 0:IMAGES]))
            dve.wait_ge(route_vec, 15)
            link(dve.scalar_tensor_tensor(out=ew[:, :], in0=ew_raw[:, :], scalar=1e-6, in1=ew_raw[:, :],
                                          op0=ALU.is_gt, op1=ALU.mult))
            dve.wait_ge(route_pe, 4)
            dve.tensor_reduce(late_w[:, 0:1], bank[7][0:1, 0:IMAGES], AX.X, ALU.add).then_inc(late_vec, 1)
            dve.wait_ge(late_vec, 1)
            dve.tensor_scalar(late_used[:, :], late_w[:, 0:1], 0.0, None, ALU.is_gt).then_inc(late_known, 1)

            def weights_of(j, tiles):
                img = j.count(2, 0)
                dve.tensor_copy(b2p[:, j.k % 2, :], b2w[:, bass.ds(img, 2)])
                dve.tensor_copy(ewp[:, j.k % 2, 0:tiles, :], ew_unit[:, 0:tiles, bass.ds(img, 2)]).then_inc(ewp_ready, 1)

            def split_z(j):
                b = j.k % 2
                src = z2T[:, bass.ds(j.count(2, 0), 2), :].rearrange("p b t -> p (b t)")
                dve.wait_ge(zp_hi_done, j.count(1, 1))
                dve.tensor_tensor(zp_lo[:, b, :], src, zp_hi[:, b, :].bitcast(F32), ALU.subtract).then_inc(zp_ready, 1)

            def add_h1(j):
                dve.wait_ge(o_ready, j.count(1, 1))
                k = j.k // 2
                dve.wait_ge(h1_loaded[j.k % 2], j.turn * 32 + 32 * (k + 1))
                until(dve, o_saved[j.k % 2], j.turn * 32 + 32 * k)
                dve.tensor_tensor(o_sb[:, j.k % 2, :, :], bank[6][0:HP, :].rearrange("p (c d) -> p c d", d=D),
                                  h1_in[:, j.k % 2, :, :], ALU.add).then_inc(o_done, 1)

            def mlp(tiles):
                def weigh(j, t):
                    dve.wait_ge(gw_hi_done, j.count(tiles, t + 1))
                    if not (j.first() and t < 4):
                        dve.wait_ge(down_done, j.count(tiles, t - 3))
                    if t == 0:
                        dve.wait_ge(ewp_ready, j.count(1, 1))
                    for b in range(2):
                        s = slice(b * PLACES, (b + 1) * PLACES)
                        lo = dve.scalar_tensor_tensor(out=gw_lo[:, t % 4, s], in0=g[:, t % 4, s],
                                                      scalar=ewp[:, j.k % 2, t, b:b + 1],
                                                      in1=gw_hi[:, t % 4, s].bitcast(F32), op0=ALU.mult,
                                                      op1=ALU.subtract)
                    lo.then_inc(gw_ready, 1)

                def pair(j):
                    for t in range(tiles):
                        weigh(j, t)
                        if t == 2 and not j.last():
                            split_z(j.plus(1))
                        if t == 4 and not j.last():
                            weights_of(j.plus(1), tiles)
                        if t == 7 and not j.first():
                            add_h1(j.plus(-1))
                    if j.last():
                        add_h1(j)
                if tiles > FT_FEW:
                    take_unit_weights(1, 6)
                dve.wait_ge(unit_weights_done, tiles // FT_FEW)
                weights_of(Pair(0, 0), tiles)
                pairs(dve, pair)

            def take_unit_weights(i, computed):
                dve.wait_ge(route_pe, computed)
                dve.tensor_copy(ew_unit[:, 8 * i:8 * i + 8, :],
                                bank[4 + i][:, :].rearrange("p (t b) -> p t b", b=IMAGES)).then_inc(unit_weights_done, 1)

            split_z(Pair(0, 0))
            dve.wait_ge(route_pe, 5)
            dve.tensor_copy(b2w[:, :], bank[6][:, 0:IMAGES])
            take_unit_weights(0, 5)
            by_use(dve, mlp)


_INS = ['x', 'L0_tok_w', 'L0_tok_b', 'L0_attn_Wq', 'L0_attn_Wkv', 'L0_attn_Wo', 'L0_ffn_router_w', 'L0_ffn_W1',
        'L0_ffn_b1', 'L0_ffn_W2', 'L0_ffn_b2']
_PARTITIONS = [(6,), (5, 1), (4, 2), (4, 1, 1), (3, 3), (3, 2, 1), (3, 1, 1, 1), (2, 2, 2), (2, 2, 1, 1),
               (2, 1, 1, 1, 1), (1, 1, 1, 1, 1, 1)]


def kernel(**inputs):
    import numpy as _np
    import concourse.bacc as _bacc
    from concourse import mybir as _mybir
    from concourse.bass_utils import run_bass_kernel_spmd as _run

    nc = _bacc.Bacc("TRN2", target_bir_lowering=False, num_devices=1)
    arrays, args = {}, []
    for name in _INS:
        a = _np.ascontiguousarray(inputs[name])
        arrays[f"in_{name}"] = a
        args.append(nc.dram_tensor(f"in_{name}", a.shape, _mybir.dt.from_np(a.dtype), kind="ExternalInput").ap())
    table = _np.zeros((PARTS, EXPERTS), dtype=_np.float32)
    for i, parts in enumerate(_PARTITIONS):
        for e, n in enumerate(parts):
            table[i, e] = n / 6
    arrays["in_part_w"] = table
    args.append(nc.dram_tensor("in_part_w", table.shape, F32, kind="ExternalInput").ap())
    out = nc.dram_tensor("out_0", (IMAGES, PLACES, D), F32, kind="ExternalOutput").ap()
    build(nc, *args, out)
    r = _run(nc, [arrays], core_ids=[0])
    return r.results[0]["out_0"]
```
